# Optimizing a Trainium2 kernel written in Bass

```python
import numpy as np
import jax
import jax.numpy as jnp

def _softmax(x, axis=-1):
    return jax.nn.softmax(x, axis=axis)

def _gelu(x):
    return jax.nn.gelu(x, approximate=True)

def _silu(x):
    return jax.nn.silu(x)

def _sigmoid(x):
    return jax.nn.sigmoid(x)

def _layernorm(x, axis=-1, eps=1e-05):
    m = jnp.mean(x, axis=axis, keepdims=True)
    v = jnp.var(x, axis=axis, keepdims=True)
    return (x - m) / jnp.sqrt(v + eps)

def _scatter_add(tgt, idx, src, axis=0):
    return tgt.at[idx].add(src)

def _segment_sum(src, seg, n):
    return jax.ops.segment_sum(src, seg, n)
kernel_name = 'mk_xattn_ffn_d2_seqx_r4_f62e88'

def setup_inputs(seed: int=0):
    np.random.seed(seed)
    _w = jnp.asarray

    def _rec_inputs():
        import jax
        import jax.numpy as jnp
        _rk = jax.random.key(seed)
        x = 7.22e-05 + 1 * jax.random.normal(jax.random.fold_in(_rk, 1), (4, 1024, 256), jnp.float32)
        _lenS = 1024 - jax.random.randint(jax.random.fold_in(_rk, 7), (4,), 0, max(1, 1024 // 4) + 1, jnp.int32)
        _lenS2 = 64 - jax.random.randint(jax.random.fold_in(_rk, 8), (4,), 0, max(1, 64 // 4) + 1, jnp.int32)
        _ctx_768P = jax.random.normal(jax.random.fold_in(_rk, 11), (4, 16, 192), jnp.float32)
        _ctx_768c = jax.random.dirichlet(jax.random.fold_in(_rk, 511), 0.3 * jnp.ones((16,), jnp.float32), (4, 64))
        _ctx_768t = jnp.einsum('bsk,bkd->bsd', _ctx_768c, _ctx_768P)
        _ctx_768t = _ctx_768t * jax.lax.rsqrt(jnp.mean(jnp.square(_ctx_768t)) + 1e-12) * 0.953939
        ctx_768 = -0.000191848 + 0.999787 * (_ctx_768t + 0.3 * jax.random.normal(jax.random.fold_in(_rk, 611), (4, 64, 192), jnp.float32))
        _validS = jnp.arange(1024)[None, :] < _lenS[:, None]
        _validS2 = jnp.arange(64)[None, :] < _lenS2[:, None]
        _causal = jnp.tril(jnp.ones((1024, 1024), dtype=bool))
        mask_BxS2_bk0 = jnp.logical_not(jnp.broadcast_to(_validS2[:, :], (4, 64)))
        return (x, ctx_768, mask_BxS2_bk0)
    x, ctx_768, mask_BxS2_bk0 = _rec_inputs()

    def _L0_xattn_setup():
        import jax, jax.numpy as jnp
        import numpy as np
        HEADS = 8
        DIM_HEAD = 64
        QUERY_DIM = 256
        CONTEXT_DIM = 192
        INNER = HEADS * DIM_HEAD
        key = jax.random.key(seed)
        ks = jax.random.split(key, 8)
        b, n, j = (4, 512, 512)
        x = jax.random.normal(ks[0], (b, n, QUERY_DIM), dtype=jnp.float32)
        context = jax.random.normal(ks[1], (b, j, CONTEXT_DIM), dtype=jnp.float32)
        mask = jax.random.randint(ks[2], (b, j), 0, 2).astype(jnp.bool_)
        W_q = jax.random.normal(ks[3], (QUERY_DIM, INNER), dtype=jnp.float32) / np.sqrt(QUERY_DIM)
        W_k = jax.random.normal(ks[4], (CONTEXT_DIM, INNER), dtype=jnp.float32) / np.sqrt(CONTEXT_DIM)
        W_v = jax.random.normal(ks[5], (CONTEXT_DIM, INNER), dtype=jnp.float32) / np.sqrt(CONTEXT_DIM)
        W_o = jax.random.normal(ks[6], (INNER, QUERY_DIM), dtype=jnp.float32) / np.sqrt(INNER)
        b_o = jax.random.normal(ks[7], (QUERY_DIM,), dtype=jnp.float32) * 0.01
        return {'x': x, 'context': context, 'mask': mask, 'W_q': W_q, 'W_k': W_k, 'W_v': W_v, 'W_o': W_o, 'b_o': b_o}
    _L0_xattn_all = _L0_xattn_setup()
    _L0_xattn_in = {k: v for k, v in _L0_xattn_all.items() if k in ('W_q', 'W_k', 'W_v', 'W_o', 'b_o')}
    del _L0_xattn_all

    def _L0_ffn_setup():
        import jax, jax.numpy as jnp
        import numpy as np
        N_EXPERTS = 8
        CAP_FACTOR = 1.25
        BATCH, SEQ, DMODEL, DFF = (4, 512, 256, 1024)
        key = jax.random.key(seed)
        k0, k1, k2, k3 = jax.random.split(key, 4)
        x = jax.random.normal(k0, (BATCH, SEQ, DMODEL), dtype=jnp.float32)
        Wr = jax.random.normal(k1, (DMODEL, N_EXPERTS), dtype=jnp.float32) * 0.02
        W1 = jax.random.normal(k2, (N_EXPERTS, DMODEL, DFF), dtype=jnp.float32) * 0.02
        W2 = jax.random.normal(k3, (N_EXPERTS, DFF, DMODEL), dtype=jnp.float32) * 0.02
        return {'x': x, 'Wr': Wr, 'W1': W1, 'W2': W2}
    _L0_ffn_all = _L0_ffn_setup()
    _L0_ffn_in = {k: v for k, v in _L0_ffn_all.items() if k in ('Wr', 'W1', 'W2')}
    del _L0_ffn_all

    def _L1_xattn_setup():
        import jax, jax.numpy as jnp
        import numpy as np
        HEADS = 16
        DIM_HEAD = 64
        QUERY_DIM = 256
        CONTEXT_DIM = 192
        INNER = HEADS * DIM_HEAD
        SCALE = DIM_HEAD ** (-0.5)
        key = jax.random.key(seed)
        ks = jax.random.split(key, 7)
        B, Sq, Skv = (4, 512, 512)
        x = jax.random.normal(ks[0], (B, Sq, QUERY_DIM), dtype=jnp.float32)
        context = jax.random.normal(ks[1], (B, Skv, CONTEXT_DIM), dtype=jnp.float32)
        w_q = jax.random.normal(ks[2], (QUERY_DIM, INNER), dtype=jnp.float32) / np.sqrt(QUERY_DIM)
        w_k = jax.random.normal(ks[3], (CONTEXT_DIM, INNER), dtype=jnp.float32) / np.sqrt(CONTEXT_DIM)
        w_v = jax.random.normal(ks[4], (CONTEXT_DIM, INNER), dtype=jnp.float32) / np.sqrt(CONTEXT_DIM)
        w_o = jax.random.normal(ks[5], (INNER, QUERY_DIM), dtype=jnp.float32) / np.sqrt(INNER)
        b_o = jax.random.normal(ks[6], (QUERY_DIM,), dtype=jnp.float32) * 0.02
        return {'x': x, 'context': context, 'w_q': w_q, 'w_k': w_k, 'w_v': w_v, 'w_o': w_o, 'b_o': b_o}
    _L1_xattn_all = _L1_xattn_setup()
    _L1_xattn_in = {k: v for k, v in _L1_xattn_all.items() if k in ('w_q', 'w_k', 'w_v', 'w_o', 'b_o')}
    del _L1_xattn_all

    def _L1_ffn_setup():
        import jax, jax.numpy as jnp
        import numpy as np
        B, S, H, I, E, K = (2, 512, 256, 512, 8, 2)
        key = jax.random.key(seed)
        k1, k2, k3, k4, k5 = jax.random.split(key, 5)
        scale_h = 1.0 / np.sqrt(H)
        scale_i = 1.0 / np.sqrt(I)
        return {'x': jax.random.normal(k1, (B, S, H), dtype=jnp.float32), 'Wg': jax.random.normal(k2, (H, E), dtype=jnp.float32) * scale_h, 'W11': jax.random.normal(k3, (E, H, I), dtype=jnp.float32) * scale_h, 'W12': jax.random.normal(k4, (E, H, I), dtype=jnp.float32) * scale_h, 'W2': jax.random.normal(k5, (E, I, H), dtype=jnp.float32) * scale_i}
    _L1_ffn_all = _L1_ffn_setup()
    _L1_ffn_in = {k: v for k, v in _L1_ffn_all.items() if k in ('Wg', 'W11', 'W12', 'W2')}
    del _L1_ffn_all
    return {'x': x, 'ctx_768': ctx_768, 'mask_BxS2_bk0': mask_BxS2_bk0, 'L0_xattn_W_q': _L0_xattn_in['W_q'], 'L0_xattn_W_k': _L0_xattn_in['W_k'], 'L0_xattn_W_v': _L0_xattn_in['W_v'], 'L0_xattn_W_o': _L0_xattn_in['W_o'], 'L0_xattn_b_o': _L0_xattn_in['b_o'], 'L0_ffn_Wr': _L0_ffn_in['Wr'], 'L0_ffn_W1': _L0_ffn_in['W1'], 'L0_ffn_W2': _L0_ffn_in['W2'], 'L1_xattn_w_q': _L1_xattn_in['w_q'], 'L1_xattn_w_k': _L1_xattn_in['w_k'], 'L1_xattn_w_v': _L1_xattn_in['w_v'], 'L1_xattn_w_o': _L1_xattn_in['w_o'], 'L1_xattn_b_o': _L1_xattn_in['b_o'], 'L1_ffn_Wg': _L1_ffn_in['Wg'], 'L1_ffn_W11': _L1_ffn_in['W11'], 'L1_ffn_W12': _L1_ffn_in['W12'], 'L1_ffn_W2': _L1_ffn_in['W2']}

def reference(x, ctx_768, mask_BxS2_bk0, L0_xattn_W_q, L0_xattn_W_k, L0_xattn_W_v, L0_xattn_W_o, L0_xattn_b_o, L0_ffn_Wr, L0_ffn_W1, L0_ffn_W2, L1_xattn_w_q, L1_xattn_w_k, L1_xattn_w_v, L1_xattn_w_o, L1_xattn_b_o, L1_ffn_Wg, L1_ffn_W11, L1_ffn_W12, L1_ffn_W2):
    import jax
    import jax.numpy as jnp

    def _L0_xattn_ref(x, context, mask, W_q, W_k, W_v, W_o, b_o):
        import jax, jax.numpy as jnp
        import numpy as np
        HEADS = 8
        DIM_HEAD = 64
        QUERY_DIM = 256
        CONTEXT_DIM = 192
        INNER = HEADS * DIM_HEAD
        b, n, _ = x.shape
        j = context.shape[1]
        scale = DIM_HEAD ** (-0.5)
        q = (x @ W_q).reshape(b, n, HEADS, DIM_HEAD)
        k = (context @ W_k).reshape(b, j, HEADS, DIM_HEAD)
        v = (context @ W_v).reshape(b, j, HEADS, DIM_HEAD)
        sim = jnp.einsum('bihd,bjhd->bhij', q, k) * scale
        max_neg = -jnp.finfo(sim.dtype).max
        sim = jnp.where(mask[:, None, None, :], sim, max_neg)
        attn = jax.nn.softmax(sim, axis=-1)
        out = jnp.einsum('bhij,bjhd->bihd', attn, v).reshape(b, n, INNER)
        return out @ W_o + b_o

    def _L0_ffn_ref(x, Wr, W1, W2):
        import jax, jax.numpy as jnp
        import numpy as np
        N_EXPERTS = 8
        CAP_FACTOR = 1.25
        BATCH, SEQ, DMODEL, DFF = (4, 512, 256, 1024)
        B, S, D = x.shape
        E = W1.shape[0]
        cap = int(CAP_FACTOR * B * S / E)
        t = x.reshape(-1, D)
        probs = jax.nn.softmax(t @ Wr, axis=-1)
        idx = jnp.argmax(probs, axis=-1)
        pmax = jnp.max(probs, axis=-1)
        onehot = jax.nn.one_hot(idx, E, dtype=jnp.int32)
        pos = jnp.sum(jnp.cumsum(onehot, axis=0) * onehot, axis=-1) - 1
        kept = pos < cap
        flat = idx * cap + jnp.minimum(pos, cap - 1)
        disp = jnp.zeros((E * cap, D), t.dtype).at[flat].add(t * kept[:, None].astype(t.dtype))
        ein = disp.reshape(E, cap, D)
        h = jax.nn.relu(jnp.einsum('ecd,edf->ecf', ein, W1))
        eout = jnp.einsum('ecf,efd->ecd', h, W2).reshape(E * cap, D)
        comb = jnp.where(kept[:, None], eout[flat], t)
        factor = jnp.where(kept, pmax, jnp.ones_like(pmax))
        out = (comb * factor[:, None]).reshape(B, S, D)
        return out

    def _L1_xattn_ref(x, context, w_q, w_k, w_v, w_o, b_o):
        import jax, jax.numpy as jnp
        import numpy as np
        HEADS = 16
        DIM_HEAD = 64
        QUERY_DIM = 256
        CONTEXT_DIM = 192
        INNER = HEADS * DIM_HEAD
        SCALE = DIM_HEAD ** (-0.5)
        B, Sq, _ = x.shape
        Skv = context.shape[1]
        q = (x @ w_q).reshape(B, Sq, HEADS, DIM_HEAD).transpose(0, 2, 1, 3)
        k = (context @ w_k).reshape(B, Skv, HEADS, DIM_HEAD).transpose(0, 2, 1, 3)
        v = (context @ w_v).reshape(B, Skv, HEADS, DIM_HEAD).transpose(0, 2, 1, 3)
        sim = jnp.einsum('bhid,bhjd->bhij', q, k) * SCALE
        attn = jax.nn.softmax(sim, axis=-1)
        out = jnp.einsum('bhij,bhjd->bhid', attn, v)
        out = out.transpose(0, 2, 1, 3).reshape(B, Sq, INNER)
        return out @ w_o + b_o

    def _L1_ffn_ref(x, Wg, W11, W12, W2):
        import jax, jax.numpy as jnp
        import numpy as np
        B, S, H, I, E, K = (2, 512, 256, 512, 8, 2)
        gate_scores = jax.nn.softmax(x @ Wg, axis=-1)
        topk_scores, topk_idx = jax.lax.top_k(gate_scores, K)
        topk_scores = topk_scores / (topk_scores.sum(-1, keepdims=True) + 1e-08)
        gate = jnp.einsum('bsh,ehi->bsei', x, W11)
        value = jnp.einsum('bsh,ehi->bsei', x, W12)
        fused = gate * jax.nn.sigmoid(gate) * value
        expert_out = jnp.einsum('bsei,eih->bseh', fused, W2)
        gathered = jnp.take_along_axis(expert_out, topk_idx[..., None], axis=2)
        out = jnp.sum(topk_scores[..., None] * gathered, axis=2)
        return out
    x = x + _L0_xattn_ref(_layernorm(x, axis=-1), ctx_768, mask_BxS2_bk0, L0_xattn_W_q, L0_xattn_W_k, L0_xattn_W_v, L0_xattn_W_o, L0_xattn_b_o)
    x = x + _L0_ffn_ref(_layernorm(x, axis=-1), L0_ffn_Wr, L0_ffn_W1, L0_ffn_W2)
    x = x + _L1_xattn_ref(_layernorm(x, axis=-1), ctx_768, L1_xattn_w_q, L1_xattn_w_k, L1_xattn_w_v, L1_xattn_w_o, L1_xattn_b_o)
    x = x + _L1_ffn_ref(_layernorm(x, axis=-1), L1_ffn_Wg, L1_ffn_W11, L1_ffn_W12, L1_ffn_W2)
    return x

_drawn_inputs = setup_inputs


def setup_inputs(seed=0):
    import zlib

    import numpy as np

    out = dict(_drawn_inputs(seed))
    spreads = {}
    factors = {}
    for name, (base, spread) in spreads.items():
        noise = np.random.default_rng([zlib.crc32(name.encode()), seed]).standard_normal(out[name].shape)
        drawn = base * np.exp(spread * noise) if base else spread * noise
        out[name] = jnp.asarray(drawn.astype(out[name].dtype))
    for name, factor in factors.items():
        out[name] = (out[name] * factor).astype(out[name].dtype)
    return out
```

```python
from contextlib import ExitStack

import numpy as np
import concourse.bass as bass
import concourse.mybir as mybir
from concourse.alu_op_type import AluOpType as ALU

F32 = mybir.dt.float32
F32R = mybir.dt.float32r
BF16 = mybir.dt.bfloat16
I32 = mybir.dt.int32
U8 = mybir.dt.uint8
ACT = mybir.ActivationFunctionType
AX = mybir.AxisListType

P = 128
B, SEQ, D = 4, 1024, 256
TOK = B * SEQ
NT = TOK // P
KC = D // P
KEYS, CTX, DH = 64, 192, 64
CP = CTX // 2
E = 8
EPS = 1e-5
BIG = -3.3895313892515355e38
G = 4
CAP = int(1.25 * TOK / E)
F0 = 1024
D0_ROWS = E * CAP + TOK
F1 = 512
T1 = 256
ROOM = TOK + T1
IDLE_ROW = E * ROOM
D1_ROWS = IDLE_ROW + T1
NT1 = (2 * TOK + E * (T1 - 1)) // T1
META = 4
DW = D + META


def is_int(v):
    return isinstance(v, (int, np.integer))


def wait(eng, sem, value):
    if not is_int(value) or value > 0:
        eng.wait_ge(sem, value)


class Chain:

    def __init__(self, eng, sem, round_, n):
        self.eng, self.sem, self.base, self.n, self.j = eng, sem, round_ * n, n, 0

    def __call__(self, ins):
        self.j += 1
        ins.then_inc(self.sem, 1)
        self.eng.wait_ge(self.sem, self.base + self.j)

    def end(self):
        assert self.j == self.n, (self.j, self.n)


class Steps:

    def __init__(self, eng, sem, round_, n, steps):
        self.eng, self.sem, self.base, self.steps, self.j = eng, sem, round_ * n, list(steps), 0

    def add_wait(self, sem, value):
        self.steps.insert(0, (sem, value))

    def more(self, n, hold=None):
        while n > 0 and self.steps:
            if isinstance(self.steps[0], tuple) and self.steps[0][0] is hold:
                return
            s = self.steps.pop(0)
            if isinstance(s, tuple):
                wait(self.eng, *s)
                continue
            if self.j:
                self.eng.wait_ge(self.sem, self.base + self.j)
            s().then_inc(self.sem, 1)
            self.j += 1
            n -= 1


class Program:
    def __init__(self, nc):
        self.nc = nc
        self.keep = ExitStack()
        self.sems = []
        self.phases = 0

    def sb(self, stack, name, shape, dt=F32):
        return stack.enter_context(self.nc.sbuf_tensor(name, shape, dt))

    def sem(self, name):
        s = self.nc.alloc_semaphore(name=name)
        self.sems.append(s)
        return s

    def phase(self):
        self.nc.clear_and_free_semaphores(self.sems)
        self.sems = []
        self.nc.all_engine_barrier()
        self.phases += 1
        self.s_land = self.sem(f"landing{self.phases}")


def constants(p, first):
    nc, k = p.nc, p.keep
    p.x = p.sb(k, "x", [P, NT, D])
    p.ident = p.sb(k, "ident", [P, P])
    p.ones_r = p.sb(k, "ones_r", [1, P], F32R)
    p.ones_b = p.sb(k, "ones_b", [P, P], BF16)
    p.below = p.sb(k, "below", [P, P], BF16)
    p.half = p.sb(k, "half", [P, 1])
    p.eps = p.sb(k, "eps", [P, 2])
    p.first8 = p.sb(k, "first8", [P, 1, E])
    p.expert8 = p.sb(k, "expert8", [P, 1, E])
    p.token = p.sb(k, "token", [P, NT])
    p.iota_i = p.sb(k, "iota_i", [P, NT], I32)
    p.bo_hi = p.sb(k, "bo_hi", [1, D], F32R)
    p.bo_lo = p.sb(k, "bo_lo", [1, D], F32R)
    p.factor0 = p.sb(k, "factor0", [P, NT])
    p.row0 = p.sb(k, "row0", [P, NT], I32)
    p.next = p.sb(k, "next_row", [P, 1, E])
    p.psum = k.enter_context(nc.psum_tensor("psum", [P, 8, 512], F32))
    p.zero = p.sb(first, "zero", [P, CAP // P * D])
    p.s_x, p.s_zero, p.s_zeroed = p.sem("x_loaded"), p.sem("zero_memset"), p.sem("zero_fill")
    s_c, s_i = p.sem("const_memset"), p.sem("const_select")
    with nc.Block() as block:
        @block.gpsimd
        def _(e):
            e.memset(p.ident[:, :], 0.0).then_inc(s_c, 1)
            e.memset(p.ones_b[:, :], 1.0).then_inc(s_c, 1)
            e.memset(p.half[:, :], -0.5)
            e.memset(p.eps[:, 0:1], 0.0)
            e.memset(p.eps[:, 1:2], EPS)
            e.wait_ge(s_c, 2)
            e.affine_select(out=p.ident[:, :], in_=p.ident[:, :], compare_op=ALU.not_equal, fill=1.0,
                            base=0, pattern=[[-1, P]], channel_multiplier=1).then_inc(s_i, 1)
            e.affine_select(out=p.below[:, :], in_=p.ones_b[:, :], compare_op=ALU.is_gt, fill=0.0,
                            base=0, pattern=[[1, P]], channel_multiplier=-1).then_inc(s_i, 1)
            e.iota(p.iota_i[:, :], pattern=[[P, NT]], base=0, channel_multiplier=1).then_inc(s_i, 1)

        @block.vector
        def _(e):
            e.memset(p.zero[:, :], 0.0).then_inc(p.s_zero, 1)
            for j in range(E):
                e.memset(p.expert8[:, :, j:j + 1], float(j))
                e.memset(p.first8[:, :, j:j + 1], float(E - j))
            e.wait_ge(s_i, 3)
            e.tensor_copy(p.token[:, :], p.iota_i[:, :])
            e.tensor_copy(p.ones_r[:, :], p.ones_b[0:1, :])


def first_loads(p, e, ins):
    for q in range(4):
        t = slice(q * NT // 4, (q + 1) * NT // 4)
        e.dma_start(p.x[:, t, :], ins["x"].rearrange("(t p) d -> p t d", p=P)[:, t, :]).then_inc(p.s_x, 16)
    e.wait_ge(p.s_zero, 1)
    for q in range(E):
        e.dma_start(p.d0[q * CAP:(q + 1) * CAP, :].rearrange("(p r) d -> p (r d)", p=P),
                    p.zero[:, :]).then_inc(p.s_zeroed, 16)
        r0, n = E * CAP + q * SEQ // 2, SEQ // 2
        e.dma_start(p.d0[r0:r0 + n, :].rearrange("(p r) d -> p (r d)", p=P),
                    p.zero[:, 0:n // P * D]).then_inc(p.s_zeroed, 16)
    e.dma_start(p.d1[IDLE_ROW:IDLE_ROW + T1, :].rearrange("(p r) d -> p (r d)", p=P),
                p.zero[:, 0:T1 // P * DW]).then_inc(p.s_zeroed, 16)
    e.dma_start(p.out[TOK:TOK + T1, :].rearrange("(p r) d -> p (r d)", p=P),
                p.zero[:, 0:T1 // P * D]).then_inc(p.s_zeroed, 16)


ZEROED = 16 * (2 * E + 2)


def attention_setup(p, layer, ins, st):
    nc = p.nc
    H = 8 if layer == 0 else 16
    PR, W, INNER = H // 2, H * KEYS, H * DH
    NB = W // 512
    n = f"L{layer}_"
    m_hi = p.sb(st, n + "m_hi", [P, B, KC, W], F32R)
    m_lo = p.sb(st, n + "m_lo", [P, B, KC, W], F32R)
    masked = p.sb(st, n + "masked", [1, B, W], BF16) if layer == 0 else None
    with ExitStack() as tmp:
        with ExitStack() as early:
            ctxT = p.sb(early, n + "ctxT", [CP, 2, B * KEYS])
            wk = p.sb(early, n + "wk", [CP, 2, INNER])
            wv = p.sb(early, n + "wv", [CP, 2, INNER])
            wqT = p.sb(early, n + "wqT", [P, PR, D])
        n_hi = p.sb(st, n + "n_hi", [P, B, PR, D], F32R)
        n_lo = p.sb(st, n + "n_lo", [P, B, PR, D], F32R)
        kd = p.sb(tmp, n + "kd", [P, PR, B, P])
        vd = p.sb(tmp, n + "vd", [P, PR, B, P])
        wo = p.sb(tmp, n + "wo", [P, PR, D])
        bo = p.sb(tmp, n + "bo", [1, D])
        if layer == 0:
            keep_u = p.sb(tmp, n + "keep_u", [P, B * KEYS], U8)
            keep = p.sb(tmp, n + "keep", [P, B, 1, KEYS])
            full = p.sb(tmp, n + "full", [P, 2, W])
        s_w, s_wo, s_zero, s_kv, s_kvc = (p.sem(n + x) for x in ("w_loaded", "wo_loaded", "kd_zero", "kv", "kv_copied"))
        s_m, s_full, s_mhi, s_mlo = (p.sem(n + x) for x in ("m", "m_masked", "m_hi", "m_lo"))
        s_n, s_nhi, s_nlo, s_keep = (p.sem(n + x) for x in ("n", "n_hi", "n_lo", "keep"))
        s_bo, s_keep_u, s_bohi = (p.sem(n + x) for x in ("bo_loaded", "mask_loaded", "bo_hi"))
        ps = p.psum
        RING_M = 2
        with nc.Block() as block:
            @block.sync
            def _(e):
                e.dma_start(ctxT[:, :, :], ins["ctxT"].rearrange("(c p) k -> p c k", p=CP)).then_inc(s_w, 16)
                e.dma_start(wk[:, :, :], ins[f"wk{layer}"].rearrange("(c p) n -> p c n", p=CP)).then_inc(s_w, 16)
                e.dma_start(wv[:, :, :], ins[f"wv{layer}"].rearrange("(c p) n -> p c n", p=CP)).then_inc(s_w, 16)
                e.dma_start(wqT[:, :, :], ins[f"wqT{layer}"].rearrange("(r p) d -> p r d", p=P)).then_inc(s_w, 16)
                e.dma_start(wo[:, :, :], ins[f"wo{layer}"].rearrange("(r p) d -> p r d", p=P)).then_inc(s_wo, 16)
                e.dma_start(bo[:, :], ins[f"bo{layer}"]).then_inc(s_bo, 16)
                if layer == 0:
                    e.dma_start(keep_u[:, :], ins["mask"].to_broadcast([P, B * KEYS])).then_inc(s_keep_u, 16)
                    first_loads(p, e, ins)

            @block.gpsimd
            def _(e):
                e.memset(vd[:, :, :, :], 0.0).then_inc(s_zero, 1)

            @block.tensor
            def _(e):
                e.wait_ge(s_w, 64)
                for j in range(2 * PR):
                    w, r = (wk, j) if j < PR else (wv, j - PR)
                    wait(e, s_kvc, j - 3)
                    for c in range(2):
                        mm = e.matmul(ps[:, j % 4, 0:B * KEYS], w[:, c, r * P:(r + 1) * P], ctxT[:, c, :],
                                      start=(c == 0), stop=(c == 1))
                    mm.then_inc(s_kv, 1)
                e.wait_ge(s_kvc, 2 * PR)
                with e.Fori(0, B) as b:
                    for c in range(KC):
                        r2 = c % RING_M
                        e.wait_ge(s_mlo, b * KC + c + 1)
                        for r in range(PR):
                            mm = e.matmul(ps[:, r2 * NB + r // 4, (r % 4) * P:(r % 4 + 1) * P],
                                          wqT[:, r, c * P:(c + 1) * P], kd[:, r, b, :], start=True, stop=True)
                        mm.then_inc(s_m, 1)
                e.wait_ge(s_wo, 16)
                for b in range(B):
                    for r in range(PR):
                        e.wait_ge(s_nlo, b * PR + r + 1)
                        e.matmul(ps[:, 4 + r % 4, 0:D], vd[:, r, b, :], wo[:, r, :],
                                 start=True, stop=True).then_inc(s_n, 1)

            @block.scalar
            def _(e):
                e.sem_inc(s_mlo, RING_M)
                e.sem_inc(s_nlo, 4)
                with e.Fori(0, B) as b:
                    for c in range(KC):
                        if layer == 0:
                            e.wait_ge(s_full, b * KC + c + 1)
                            src, scale = full[:, c, :], 1.0
                        else:
                            e.wait_ge(s_m, b * KC + c + 1)
                            src, scale = ps[:, c * NB:(c + 1) * NB, :].rearrange("p a b -> p (a b)"), 0.125
                        e.sem_inc(p.s_land, 1)
                        e.activation(m_hi[:, b, c, :], src, ACT.Copy, scale=scale).then_inc(s_mhi, 1)
                with e.Fori(0, B) as b:
                    for r in range(PR):
                        e.wait_ge(s_n, b * PR + r + 1)
                        e.sem_inc(p.s_land, 1)
                        e.activation(n_hi[:, b, r, :], ps[:, 4 + r % 4, 0:D], ACT.Copy).then_inc(s_nhi, 1)

            @block.vector
            def _(e):
                e.memset(kd[:, :, :, :], 0.0).then_inc(s_zero, 1)
                for j in range(E):
                    e.memset(p.next[:, :, j:j + 1], float(j * (CAP if layer == 0 else ROOM)))
                e.wait_ge(s_zero, 2)
                for j in range(2 * PR):
                    d, r = (kd, j) if j < PR else (vd, j - PR)
                    e.wait_ge(s_kv, j + 1)
                    for h in range(2):
                        q = slice(h * DH, (h + 1) * DH)
                        cp = e.tensor_copy(d[q, r, :, h * KEYS:(h + 1) * KEYS],
                                           ps[q, j % 4, 0:B * KEYS].rearrange("p (b k) -> p b k", b=B))
                    cp.then_inc(s_kvc, 1)
                e.wait_ge(s_bo, 16)
                e.tensor_copy(p.bo_hi[:, :], bo[:, :]).then_inc(s_bohi, 1)
                e.wait_ge(s_bohi, 1)
                e.tensor_tensor(p.bo_lo[:, :], bo[:, :], p.bo_hi[:, :].bitcast(F32), ALU.subtract)
                if layer == 0:
                    e.wait_ge(s_keep_u, 16)
                    e.tensor_copy(keep[:, :, 0, :], keep_u[:, :].rearrange("p (b k) -> p b k", b=B)).then_inc(s_keep, 1)
                    e.wait_ge(s_keep, 1)
                    for b in range(B):
                        e.tensor_scalar(masked[:, b, :].rearrange("p (h k) -> p h k", h=H),
                                        keep[0:1, b, :, :].to_broadcast([1, H, KEYS]),
                                        -BIG, BIG, ALU.mult, ALU.add)
                with e.Fori(0, B) as b:
                    for c in range(KC):
                        if layer == 0:
                            e.wait_ge(s_m, b * KC + c + 1)
                            e.scalar_tensor_tensor(full[:, c, :].rearrange("p (h k) -> p h k", h=H),
                                                   ps[:, c, :].rearrange("p (h k) -> p h k", h=H), 0.125,
                                                   keep[:, b, :, :].to_broadcast([P, H, KEYS]),
                                                   ALU.mult, ALU.mult).then_inc(s_full, 1)
                            e.wait_ge(s_mhi, b * KC + c + 1)
                            e.tensor_tensor(m_lo[:, b, c, :], full[:, c, :], m_hi[:, b, c, :].bitcast(F32),
                                            ALU.subtract).then_inc(s_mlo, 1)
                        else:
                            e.wait_ge(s_mhi, b * KC + c + 1)
                            e.scalar_tensor_tensor(m_lo[:, b, c, :],
                                                   ps[:, c * NB:(c + 1) * NB, :].rearrange("p a b -> p (a b)"),
                                                   0.125, m_hi[:, b, c, :].bitcast(F32),
                                                   ALU.mult, ALU.subtract).then_inc(s_mlo, 1)
                with e.Fori(0, B) as b:
                    for r in range(PR):
                        e.wait_ge(s_nhi, b * PR + r + 1)
                        e.tensor_tensor(n_lo[:, b, r, :], ps[:, 4 + r % 4, 0:D], n_hi[:, b, r, :].bitcast(F32),
                                        ALU.subtract).then_inc(s_nlo, 1)
    return m_hi, m_lo, n_hi, n_lo, masked


def attention(p, layer, ins, mats, st):
    nc, ps = p.nc, p.psum
    m_hi, m_lo, n_hi, n_lo, masked = mats
    H = 8 if layer == 0 else 16
    CH = 1 if layer == 0 else 2
    RA = 7 if layer == 0 else 13
    NR = 22 if layer == 0 else 30
    PR, W = H // 2, H * KEYS
    NB = W // 512
    n = f"L{layer}_"
    wr = p.sb(st, n + "wr", [P, KC, E])
    xn = p.sb(st, n + "xn", [P, 2, D])
    xT_hi = p.sb(st, n + "xT_hi", [P, 2, KC, P], F32R)
    xT_lo = p.sb(st, n + "xT_lo", [P, 2, KC, P], F32R)
    prob = p.sb(st, n + "prob", [P, 2, W])
    pT_hi = p.sb(st, n + "pT_hi", [P, PR, P], F32R)
    pT_lo = p.sb(st, n + "pT_lo", [P, PR, P], F32R)
    xf = p.sb(st, n + "xf", [P, 2, D])
    xfT = p.sb(st, n + "xfT", [P, KC, P])
    stage = p.sb(st, n + "stage", [P, G, DW])
    tails = p.sb(st, n + "tails", [P, 2 * G, META])
    rowf = p.sb(st, n + "rowf", [P, 2 * G, CH])
    row = p.sb(st, n + "row", [P, G, CH], I32)
    nmx, sm, rc = (p.sb(st, n + x, [P, 2, H, 1]) for x in ("neg_max", "sum", "rcp"))
    stats = p.sb(st, n + "stats", [P, 2, 6])
    mv1 = p.sb(st, n + "mv1", [P, G, 2])
    mv2 = p.sb(st, n + "mv2", [P, G, 2])
    mv = p.sb(st, n + "mv", [P, NT, 2])
    rs1 = p.sb(st, n + "rs1", [P, G])
    rs2 = p.sb(st, n + "rs2", [P, NT])
    nb2 = p.sb(st, n + "nb2", [P, NT])
    lg = p.sb(st, n + "lg", [P, G, E])
    sh, sh2, ex, a1, oh1, a2, oh2, pos, c1, c2 = (p.sb(st, n + x, [P, G, E]) for x in
                                                  ("sh", "sh2", "ex", "a1", "oh1", "a2", "oh2", "pos", "c1", "c2"))
    oh_b = p.sb(st, n + "oh_b", [P, G, E], BF16)
    ranks = p.sb(st, n + "ranks", [P, G + 1, E])
    f1, r1, r2, r3, r4, r5 = (p.sb(st, n + x, [P, G, 1]) for x in ("f1", "r1", "r2", "r3", "r4", "r5"))
    if layer == 1:
        got = p.sb(st, n + "got", [P, G, D])
        gidx = p.sb(st, n + "gidx", [P, G], I32)

    S = lambda name: p.sem(n + name)
    s_wr = S("wr_loaded")
    s_gidx, s_got = S("gather_index"), [S(f"gathered{j}") for j in range(G)]
    s_cmb, s_st1, s_ch1, s_rs1, s_eps1 = S("combined"), S("stats1"), S("bn1"), S("rstd1"), S("eps1")
    s_xn, s_xT, s_xThi, s_xTlo = S("xn"), S("xT"), S("xT_hi"), S("xT_lo")
    s_sim, s_mx, s_exp, s_rcp, s_p = (S(x) for x in ("scores", "max", "exp", "reciprocal", "prob"))
    s_pT, s_pThi, s_pTlo, s_out, s_res = (S(x) for x in ("pT", "pT_hi", "pT_lo", "output", "residual"))
    s_ch2, s_st2, s_rs2, s_eps2, s_nb2, s_xf, s_xfT, s_xfTc, s_lgp, s_lg = (
        S(x) for x in ("bn2", "stats2", "rstd2", "eps2", "neg_mean2", "xf", "xfT", "xfT_copied", "logits", "logits_copied"))
    s_route, s_rexp, s_pos, s_posr = (S(x) for x in ("routing", "route_exp", "ranks", "ranks_copied"))
    s_stg, s_scat, s_store = S("staged"), [S(f"scattered{j}") for j in range(G)], S("x_stored")

    S_BANK, T_BANK, O_BANK, X_BANK = 0, 4, 6, 7
    LOGITS = slice(0, E)
    RANKS = slice(256, 256 + (G + 1) * E)
    ok = lambda t: not is_int(t) or 0 <= t < NT
    okg = lambda g: not is_int(g) or 0 <= g < NT // G
    flat = lambda ap: ap.rearrange("p a b -> p (a b)")
    col = lambda ap, t: ap[:, t:t + 1] if is_int(t) else ap[:, bass.ds(t, 1)]

    def scores_ps(k):
        return flat(ps[:, S_BANK + (k % 2) * NB:S_BANK + (k % 2 + 1) * NB, :])

    def pT_ps():
        return flat(ps[:, T_BANK:T_BANK + NB, :])

    def cap(t, last=NT):
        return min(t, last) if is_int(t) else t

    def run(eng, body):
        for g in (-2, -1, 0, 1, 2):
            body(g)
        with eng.Fori(3, 6) as g:
            body(g)
        for g in (6, 7, 8, 9):
            body(g)

    def land(eng, t=None):
        if not is_int(t):
            eng.sem_inc(p.s_land, 1)

    with nc.Block() as block:
        @block.sync
        def _(e):
            e.dma_start(wr[:, :, :], ins[f"wr{layer}"].rearrange("(c p) e -> p c e", p=P)).then_inc(s_wr, 16)
            if layer == 1:
                out_t = p.out[0:TOK, :].rearrange("(t p) d -> p t d", p=P)
                with e.Fori(0, NT) as t:
                    e.wait_ge(s_res, t + 1)
                    e.dma_start(out_t[:, t, :], p.x[:, t, :]).then_inc(s_store, 16)
                e.wait_ge(s_store, 16 * NT)

        def pe_body(e, g):
            if is_int(g):
                seq = (g // 2, (g + 1) // 2)
            else:
                seq = tuple(e.snap(v >> 1, min_val=0, max_val=B - 1) for v in (g, g + 1))
            for k in range(G):
                t = g * G + k
                if ok(t):
                    wait(e, s_p, t + 1)
                    wait(e, s_pTlo, t)
                    for r in range(PR):
                        mm = e.transpose(ps[:, T_BANK + r // 4, (r % 4) * P:(r % 4 + 1) * P],
                                         prob[:, k % 2, r * P:(r + 1) * P], p.ident[:, :])
                    mm.then_inc(s_pT, 1)
                if ok(t + 4) or ok(t - 2):
                    wait(e, s_xTlo, cap(t + 4))
                    wait(e, s_lg, cap(t - 2))
                if ok(t + 4):
                    wait(e, s_xn, t + 5)
                    for c in range(KC):
                        mm = e.transpose(ps[:, X_BANK, c * P:(c + 1) * P], xn[:, k % 2, c * P:(c + 1) * P],
                                         p.ident[:, :])
                    mm.then_inc(s_xT, 1)
                if ok(t - 2):
                    wait(e, s_xf, t - 1)
                    for c in range(KC):
                        mm = e.transpose(ps[:, X_BANK, 256 + c * P:256 + (c + 1) * P],
                                         xf[:, k % 2, c * P:(c + 1) * P], p.ident[:, :])
                    mm.then_inc(s_xfT, 1)
                if k == 3 and okg(g - 1):
                    wait(e, s_route, (g - 1) * NR + RA)
                    wait(e, s_res, cap(t))
                    rk = lambda j: ps[:, O_BANK, 256 + j * E:256 + G * E]
                    e.matmul(rk(0), p.below[:, :], flat(oh_b[:, :, :]), start=True, stop=False)
                    for j in range(1, G):
                        e.matmul(rk(j), p.ones_b[:, :], flat(oh_b[:, 0:G - j, :]), start=False, stop=(j == G - 1))
                    for j in range(G):
                        mm = e.matmul(ps[:, O_BANK, 256 + G * E:256 + (G + 1) * E], p.ones_b[:, :], oh_b[:, j, :],
                                      start=(j == 0), stop=(j == G - 1))
                    mm.then_inc(s_pos, 1)
                if ok(t + 3):
                    b = seq[(k + 3) // G]
                    wait(e, s_xTlo, t + 4)
                    wait(e, s_exp, t + 2)
                    land(e, t)
                    for q in range(NB):
                        bank = ps[:, S_BANK + ((k + 1) % 2) * NB + q, :]
                        if layer == 0:
                            e.matmul(bank, p.ones_b[0:1, :], masked[:, b, :], start=True, stop=False)
                        for c in range(KC):
                            for j, (a, m) in enumerate(((xT_hi, m_hi), (xT_lo, m_hi), (xT_hi, m_lo))):
                                mm = e.matmul(bank, a[:, (k + 1) % 2, c, :], m[:, b, c, q * 512:(q + 1) * 512],
                                              start=(layer == 1 and c == 0 and j == 0),
                                              stop=(c == KC - 1 and j == 2))
                    mm.then_inc(s_sim, 1)
                if ok(t):
                    b = seq[0]
                    wait(e, s_res, t)
                    if k == 3:
                        wait(e, s_posr, g)
                    o = ps[:, O_BANK, 0:D]
                    e.matmul(o, p.ones_r[:, :], p.bo_hi[:, :], start=True, stop=False)
                    e.matmul(o, p.ones_r[:, :], p.bo_lo[:, :], start=False, stop=False)
                    wait(e, s_pTlo, t + 1)
                    land(e, t)
                    for r in range(PR):
                        for j, (a, m) in enumerate(((pT_hi, n_hi), (pT_lo, n_hi), (pT_hi, n_lo))):
                            mm = e.matmul(o, a[:, r, :], m[:, b, r, :], start=False, stop=(r == PR - 1 and j == 2))
                    mm.then_inc(s_out, 1)
                if ok(t - 2):
                    wait(e, s_xfTc, t - 1)
                    wait(e, s_xTlo, cap(t + 5))
                    for c in range(KC):
                        mm = e.matmul(ps[:, X_BANK, LOGITS], xfT[:, c, :], wr[:, c, :], start=(c == 0), stop=(c == KC - 1))
                    mm.then_inc(s_lgp, 1)

        @block.tensor
        def _(e):
            e.wait_ge(s_wr, 16)
            run(e, lambda g: pe_body(e, g))

        def act_body(e, g):
            for k in range(G):
                t = g * G + k
                if ok(t):
                    wait(e, s_pT, t + 1)
                    e.activation(flat(pT_hi[:, :, :]), pT_ps(), ACT.Copy).then_inc(s_pThi, 1)
                if ok(t + 4):
                    wait(e, s_xT, t + 5)
                    wait(e, s_xfT, cap(t - 1))
                    e.activation(flat(xT_hi[:, k % 2, :, :]), ps[:, X_BANK, 0:D], ACT.Copy).then_inc(s_xThi, 1)
                if ok(t - 2):
                    wait(e, s_xfT, t - 1)
                    e.activation(flat(xfT[:, :, :]), ps[:, X_BANK, 256:512], ACT.Copy).then_inc(s_xfTc, 1)
                if k == 2 and okg(g - 1):
                    wait(e, s_route, (g - 1) * NR + 2)
                    e.activation(ex[:, :, :], sh[:, :, :], ACT.Exp).then_inc(s_rexp, 1)
                if ok(t - 8):
                    slot = (g % 2) * G + k
                    wait(e, s_route, (g - 1) * NR)
                    wait(e, s_nb2, t - 7)
                    wait(e, s_scat[k], 16 * CH * (g - 2))
                    land(e)
                    e.activation(stage[:, k, 0:D], p.x[:, t - 8, :], ACT.Identity, bias=col(nb2, t - 8),
                                 scale=col(rs2, t - 8))
                    if layer == 1:
                        e.activation(stage[:, k, D:DW], tails[:, slot, :], ACT.Copy)
                    e.activation(row[:, k, :], rowf[:, slot, :], ACT.Copy).then_inc(s_stg, 1)
                if ok(t + 2):
                    q = k % 2
                    wait(e, s_mx, t + 3)
                    wait(e, s_pT, t + 1)
                    for h in range(H):
                        last = e.activation(prob[:, q, h * KEYS:(h + 1) * KEYS], scores_ps(k)[:, h * KEYS:(h + 1) * KEYS],
                                            ACT.Exp, bias=nmx[:, q, h, :], accum_out=sm[:, q, h, :])
                    last.then_inc(s_exp, 1)

        @block.scalar
        def _(e):
            run(e, lambda g: act_body(e, g))

        def pool_body(e, g):
            for k in range(G):
                t = g * G + k
                if layer == 1 and ok(t + 8):
                    wait(e, s_cmb, t + 5)
                    land(e, t)
                    e.tensor_copy(gidx[:, k:k + 1], p.row0[:, bass.ds(t + 8, 1)]).then_inc(s_gidx, 1)
                    wait(e, s_gidx, t + 9)
                    land(e, t)
                    e.indirect_dma_start(got[:, k, :], None, p.d0[:, :],
                                         bass.IndirectOffsetOnAxis(ap=gidx[:, k:k + 1], axis=0)).then_inc(s_got[k], 16)
                if ok(t + 1):
                    q = (k + 1) % 2
                    wait(e, s_rcp, t + 2)
                    pr = prob[:, q, :].rearrange("p (h k) -> p h k", h=H)
                    e.tensor_tensor(pr, pr, rc[:, q, :, :].to_broadcast([P, H, KEYS]), ALU.mult).then_inc(s_p, 1)
                if layer == 0 and is_int(t) and t == 8:
                    e.wait_ge(p.s_zeroed, ZEROED)
                if ok(t - 8):
                    wait(e, s_stg, t - 7)
                    land(e, t)
                    for c in range(CH):
                        dst = p.d0 if layer == 0 else p.d1
                        width = D if layer == 0 else DW
                        e.indirect_dma_start(dst[:, :], bass.IndirectOffsetOnAxis(ap=row[:, k, c:c + 1], axis=0),
                                             stage[:, k, 0:width], None).then_inc(s_scat[k], 16)
                q = (k + 2) % G
                if ok(t + 6):
                    wait(e, s_st1, t + 7)
                    e.tensor_tensor(mv1[:, q, :], mv1[:, q, :], p.eps[:, :], ALU.add).then_inc(s_eps1, 1)
                if ok(t):
                    wait(e, s_st2, t + 1)
                    land(e, t)
                    e.tensor_tensor(mv[:, t, :], mv2[:, k, :], p.eps[:, :], ALU.add).then_inc(s_eps2, 1)
                if ok(t + 6):
                    wait(e, s_eps1, t + 7)
                    e.tensor_tensor(rs1[:, q:q + 1], mv1[:, q, 1:2], p.half[:, :], ALU.pow).then_inc(s_rs1, 1)
                if ok(t):
                    wait(e, s_eps2, t + 1)
                    land(e, t)
                    e.tensor_tensor(col(rs2, t), mv[:, t, 1:2], p.half[:, :], ALU.pow).then_inc(s_rs2, 1)

        @block.gpsimd
        def _(e):
            run(e, lambda g: pool_body(e, g))
            for r in range(G):
                e.wait_ge(s_scat[r], 16 * CH * NT // G)

        def routing(e, gg, par):
            bc = [P, G, E]
            TT, TS, STT, RED = e.tensor_tensor, e.tensor_scalar, e.scalar_tensor_tensor, e.tensor_reduce
            slots = slice(par, par + G) if is_int(par) else bass.ds(par, G)
            gs = slice(gg * G, gg * G + G) if is_int(gg) else bass.ds(gg * G, G)
            tok = p.token[:, gs]
            steps = [lambda: RED(r1[:, :, 0], lg[:, :, :], AX.X, ALU.max),
                     lambda: TT(sh[:, :, :], lg[:, :, :], r1[:, :, :].to_broadcast(bc), ALU.subtract),
                     lambda: TS(a1[:, :, :], sh[:, :, :], 0.0, None, ALU.is_equal),
                     lambda: TT(a1[:, :, :], a1[:, :, :], p.first8[:, :, :].to_broadcast(bc), ALU.mult),
                     lambda: RED(f1[:, :, 0], a1[:, :, :], AX.X, ALU.max),
                     lambda: TT(oh1[:, :, :], a1[:, :, :], f1[:, :, :].to_broadcast(bc), ALU.is_equal)]
            if layer == 1:
                steps += [lambda: STT(flat(sh2[:, :, :]), flat(oh1[:, :, :]), BIG, flat(sh[:, :, :]), ALU.mult, ALU.add),
                          lambda: RED(r1[:, :, 0], sh2[:, :, :], AX.X, ALU.max),
                          lambda: TT(a2[:, :, :], sh2[:, :, :], r1[:, :, :].to_broadcast(bc), ALU.is_equal),
                          lambda: TT(a2[:, :, :], a2[:, :, :], p.first8[:, :, :].to_broadcast(bc), ALU.mult),
                          lambda: RED(r1[:, :, 0], a2[:, :, :], AX.X, ALU.max),
                          lambda: TT(oh2[:, :, :], a2[:, :, :], r1[:, :, :].to_broadcast(bc), ALU.is_equal),
                          lambda: TT(oh_b[:, :, :], oh1[:, :, :], oh2[:, :, :], ALU.add)]
            else:
                steps += [lambda: e.tensor_copy(oh_b[:, :, :], oh1[:, :, :])]
            assert len(steps) == RA
            steps += [(s_rexp, gg + 1),
                      lambda: RED(r1[:, :, 0], ex[:, :, :], AX.X, ALU.add)]
            if layer == 0:
                steps += [lambda: TS(r4[:, :, :], f1[:, :, :], -float(CAP), float((E + 1) * CAP), ALU.mult, ALU.add),
                          lambda: e.reciprocal(r2[:, :, :], r1[:, :, :]),
                          lambda: TS(r5[:, :, 0], tok, float(E * CAP), None, ALU.add)]
            else:
                steps += [lambda: e.reciprocal(r2[:, :, :], r1[:, :, :]),
                          lambda: TT(a2[:, :, :], ex[:, :, :], oh2[:, :, :], ALU.mult),
                          lambda: RED(r3[:, :, 0], a2[:, :, :], AX.X, ALU.add),
                          lambda: TT(r3[:, :, :], r3[:, :, :], r2[:, :, :], ALU.mult),
                          lambda: STT(r4[:, :, :], r2[:, :, :], 1e-8, r3[:, :, :], ALU.add, ALU.add),
                          lambda: e.reciprocal(r4[:, :, :], r4[:, :, :]),
                          lambda: TT(tails[:, slots, 0:1], r2[:, :, :], r4[:, :, :], ALU.mult),
                          lambda: TT(tails[:, slots, 1:2], r3[:, :, :], r4[:, :, :], ALU.mult),
                          lambda: TS(tails[:, slots, 2], tok, -float(TOK + T1), None, ALU.add),
                          lambda: e.tensor_copy(tails[:, slots, 3:4], f1[:, :, :])]
            steps += [(s_posr, gg + 1),
                      lambda: TT(pos[:, :, :], ranks[:, 0:G, :], p.next[:, :, :].to_broadcast(bc), ALU.add),
                      lambda: TT(p.next[:, :, :], p.next[:, :, :], ranks[:, G:G + 1, :], ALU.add),
                      lambda: TT(c1[:, :, :], pos[:, :, :], oh1[:, :, :], ALU.mult)]
            if layer == 0:
                steps += [lambda: RED(r3[:, :, 0], c1[:, :, :], AX.X, ALU.add),
                          lambda: TT(r4[:, :, :], r3[:, :, :], r4[:, :, :], ALU.is_lt),
                          lambda: TT(r3[:, :, :], r3[:, :, :], r5[:, :, :], ALU.subtract),
                          lambda: TT(r3[:, :, :], r3[:, :, :], r4[:, :, :], ALU.mult),
                          lambda: STT(r2[:, :, 0], r2[:, :, 0], -1.0, r4[:, :, 0], ALU.add, ALU.mult),
                          lambda: TS(p.factor0[:, gs], r2[:, :, 0], 1.0, None, ALU.add),
                          lambda: TT(p.row0[:, gs], r3[:, :, 0], r5[:, :, 0], ALU.add),
                          lambda: TT(rowf[:, slots, :], r3[:, :, :], r5[:, :, :], ALU.add)]
            else:
                steps += [lambda: TT(c2[:, :, :], pos[:, :, :], oh2[:, :, :], ALU.mult),
                          lambda: RED(rowf[:, slots, 0], c1[:, :, :], AX.X, ALU.add),
                          lambda: RED(rowf[:, slots, 1], c2[:, :, :], AX.X, ALU.add)]
            return Steps(e, s_route, gg, NR, steps)

        def dve_body(e, g):
            route = routing(e, g - 1, ((g - 1) % 2 if is_int(g) else (g + 1) % 2) * G) if okg(g - 1) else None
            for k in range(G):
                t = g * G + k
                hold = s_posr
                more = lambda n: route.more(n, hold) if route and k >= 2 else None
                late = lambda n: route.more(n, hold) if route and k >= 1 else None
                each = 1
                if ok(t + 2):
                    wait(e, s_sim, t + 3)
                    e.tensor_reduce(nmx[:, k % 2, :, 0], scores_ps(k).rearrange("p (h k) -> p h k", h=H), AX.X,
                                    ALU.max, negate=True).then_inc(s_mx, 1)
                more(each)
                if ok(t):
                    wait(e, s_pThi, t + 1)
                    e.tensor_tensor(flat(pT_lo[:, :, :]), pT_ps(), flat(pT_hi[:, :, :]).bitcast(F32),
                                    ALU.subtract).then_inc(s_pTlo, 1)
                if k == 3 and route:
                    wait(e, s_pos, g)
                    e.tensor_copy(flat(ranks[:, :, :]), ps[:, O_BANK, RANKS]).then_inc(s_posr, 1)
                    hold = None
                more(each)
                if ok(t + 4):
                    wait(e, s_xThi, t + 5)
                    wait(e, s_xfTc, cap(t - 1))
                    e.tensor_tensor(flat(xT_lo[:, k % 2, :, :]), ps[:, X_BANK, 0:D],
                                    flat(xT_hi[:, k % 2, :, :]).bitcast(F32), ALU.subtract).then_inc(s_xTlo, 1)
                more(each)
                if ok(t + 1):
                    q = (k + 1) % 2
                    wait(e, s_exp, t + 2)
                    wait(e, s_p, t)
                    e.reciprocal(rc[:, q, :, :], sm[:, q, :, :]).then_inc(s_rcp, 1)
                more(each)
                if ok(t + 5):
                    q = (k + 1) % G
                    wait(e, s_rs1, t + 6)
                    wait(e, s_xT, t + 4)
                    e.tensor_scalar(xn[:, (k + 1) % 2, :], p.x[:, t + 5, :], mv1[:, q, 0:1], rs1[:, q:q + 1],
                                    ALU.subtract, ALU.mult).then_inc(s_xn, 1)
                more(each)
                if ok(t - 1):
                    wait(e, s_rs2, t)
                    wait(e, s_xfT, t - 2)
                    e.tensor_scalar(xf[:, (k + 1) % 2, :], p.x[:, t - 1, :], mv[:, t - 1, 0:1], col(rs2, t - 1),
                                    ALU.subtract, ALU.mult).then_inc(s_xf, 1)
                    e.scalar_tensor_tensor(col(nb2, t - 1), mv[:, t - 1, 0:1], -1.0, col(rs2, t - 1),
                                           ALU.mult, ALU.mult).then_inc(s_nb2, 1)
                more(each)
                q = (k + 2) % G
                x6 = p.x[:, t + 6, :] if ok(t + 6) else None
                if ok(t + 6) and layer == 1:
                    wait(e, s_got[q], 16 * (g + (2 if k < 2 else 3)))
                    e.scalar_tensor_tensor(x6, got[:, q, :], col(p.factor0, t + 6), x6, ALU.mult, ALU.add).then_inc(s_cmb, 1)
                more(each)
                if ok(t):
                    wait(e, s_out, t + 1)
                    e.tensor_tensor(p.x[:, t, :], ps[:, O_BANK, 0:D], p.x[:, t, :], ALU.add).then_inc(s_res, 1)
                if ok(t - 2):
                    wait(e, s_lgp, t - 1)
                    e.tensor_copy(lg[:, (k - 2) % G, :], ps[:, X_BANK, LOGITS]).then_inc(s_lg, 1)
                if k == 1 and route:
                    route.add_wait(s_lg, t - 1)
                late(each)
                if ok(t + 6):
                    if layer == 1:
                        wait(e, s_cmb, t + 7)
                        land(e, t)
                    e.bn_stats(stats[:, 0, :], x6).then_inc(s_ch1, 1)
                late(each)
                if ok(t):
                    wait(e, s_res, t + 1)
                    land(e, t)
                    e.bn_stats(stats[:, 1, :], p.x[:, t, :]).then_inc(s_ch2, 1)
                late(each)
                if ok(t + 6):
                    wait(e, s_ch1, t + 7)
                    land(e, t)
                    e.bn_aggr(mv1[:, q, :], stats[:, 0, :]).then_inc(s_st1, 1)
                late(each)
                if ok(t):
                    wait(e, s_ch2, t + 1)
                    land(e, t)
                    e.bn_aggr(mv2[:, k, :], stats[:, 1, :]).then_inc(s_st2, 1)
                if k == 3 and route:
                    route.more(NR)
                    assert route.j == NR, route.j

        @block.vector
        def _(e):
            if layer == 0:
                e.wait_ge(p.s_x, 16 * 4)
            run(e, lambda g: dve_body(e, g))


def experts_capacity(p, ins):
    nc, ps = p.nc, p.psum
    FC, TC = F0 // P, CAP // P
    HALVES = ((0, 3), (3, 2))
    n = "E0_"
    with ExitStack() as st:
        w1 = p.sb(st, n + "w1", [P, KC, F0])
        w2 = p.sb(st, n + "w2", [P, FC, D])
        w1_hi, w1_lo = (p.sb(st, n + x, [P, 2, KC, F0], F32R) for x in ("w1_hi", "w1_lo"))
        w2_hi, w2_lo = (p.sb(st, n + x, [P, 2, FC, D], F32R) for x in ("w2_hi", "w2_lo"))
        xin = p.sb(st, n + "xin", [P, TC, D])
        xT_hi, xT_lo = (p.sb(st, n + x, [P, KC, CAP], F32R) for x in ("xT_hi", "xT_lo"))
        h_hi, h_lo = (p.sb(st, n + x, [P, 2, FC, 3 * P], F32R) for x in ("h_hi", "h_lo"))
        y = p.sb(st, n + "y", [P, 2, 3, D])
        S = lambda name: p.sem(n + name)
        s_w1, s_w2, s_x = S("w1_loaded"), S("w2_loaded"), S("x_loaded")
        s_w1hi, s_w1lo, s_w2hi, s_w2lo, s_used = S("w1_hi"), S("w1_lo"), S("w2_hi"), S("w2_lo"), S("weights_used")
        s_xT, s_xThi, s_xTlo, s_up = S("xT"), S("xT_hi"), S("xT_lo"), S("up")
        s_hhi, s_hlo, s_dn, s_y, s_st = S("h_hi"), S("h_lo"), S("down"), S("y_copied"), [S("y_stored0"), S("y_stored1")]
        w1_d = ins["w1"].rearrange("e (c p) f -> p e c f", p=P)
        w2_d = ins["w2"].rearrange("e (m p) d -> p e m d", p=P)
        rows = p.d0[0:E * CAP, :].rearrange("(e c p) d -> p e c d", p=P, c=TC)
        UP_BANK, X_BANK, Y_BANK = 0, 4, 6

        def pairs(eng, body):
            body(0, 0)
            body(1, 1)
            with eng.Fori(1, E // 2 - 1) as j:
                body(2 * j, 0)
                body(2 * j + 1, 1)
            body(E - 2, 0)
            body(E - 1, 1)

        def load(q, e):
            wait(q, s_w1lo, e)
            q.dma_start(w1[:, :, :], w1_d[:, e, :, :]).then_inc(s_w1, 16)
            wait(q, s_w2lo, e)
            q.dma_start(w2[:, :, :], w2_d[:, e, :, :]).then_inc(s_w2, 16)
            wait(q, s_xT, TC * e)
            q.dma_start(xin[:, :, :], rows[:, e, :, :]).then_inc(s_x, 16)

        with nc.Block() as block:
            @block.sync
            def _(q):
                load(q, 0)
                def body(e, par, last=False):
                    if not last:
                        load(q, e + 1)
                    for h, (c0, cn) in enumerate(HALVES):
                        q.wait_ge(s_y, TC * e + c0 + cn)
                        q.dma_start(rows[:, e, c0:c0 + cn, :], y[:, h, 0:cn, :]).then_inc(s_st[h], 16)
                body(0, 0)
                with q.Fori(1, E - 1) as e:
                    body(e, 0)
                body(E - 1, 0, True)
                for h in range(2):
                    q.wait_ge(s_st[h], 16 * E)

            def transposes(q, e, c0, c1):
                if c0 == 0:
                    q.wait_ge(s_x, 16 * (e + 1))
                for c in range(c0, c1):
                    wait(q, s_xTlo, TC * e + c + (0, -2, -1, -1, -1)[c])
                    for kc in range(KC):
                        mm = q.transpose(ps[:, X_BANK + bank_of(e, c), kc * P:(kc + 1) * P],
                                         xin[:, c, kc * P:(kc + 1) * P], p.ident[:, :])
                    mm.then_inc(s_xT, 1)

            def bank_of(e, c):
                return c % 2

            @block.tensor
            def _(q):
                transposes(q, 0, 0, TC)

                def up(e, par, h):
                    c0, cn = HALVES[h]
                    q.wait_ge(s_xTlo, TC * e + TC)
                    if h == 0:
                        q.wait_ge(s_w1lo, e + 1)
                    for m in range(FC):
                        i = (2 * e + h) * FC + m
                        wait(q, s_hlo, i - 3)
                        bank = ps[:, UP_BANK + m % 4, 0:cn * P]
                        k = 0
                        for c in range(KC):
                            for a, x in ((w1_hi, xT_hi), (w1_hi, xT_lo), (w1_lo, xT_hi)):
                                mm = q.matmul(bank, a[:, par, c, m * P:(m + 1) * P], x[:, c, c0 * P:(c0 + cn) * P],
                                              start=(k == 0), stop=(k == 3 * KC - 1))
                                k += 1
                        mm.then_inc(s_up, 1)

                def down(e, par, h):
                    c0, cn = HALVES[h]
                    if h == 0:
                        q.wait_ge(s_w2lo, e + 1)
                    q.wait_ge(s_hlo, (2 * e + h + 1) * FC)
                    for c in range(cn):
                        i = TC * e + c0 + c
                        wait(q, s_y, i - 1)
                        bank = ps[:, Y_BANK + (c0 + c + par) % 2, 0:D]
                        k = 0
                        for m in range(FC):
                            for a, w in ((h_hi, w2_hi), (h_lo, w2_hi), (h_hi, w2_lo)):
                                mm = q.matmul(bank, a[:, h, m, c * P:(c + 1) * P], w[:, par, m, :],
                                              start=(k == 0), stop=(k == 3 * FC - 1))
                                k += 1
                        mm.then_inc(s_dn, 1)
                    if h == 1:
                        pass

                def body(e, par, last=False):
                    up(e, par, 0)
                    up(e, par, 1)
                    down(e, par, 0)
                    if not last:
                        transposes(q, e + 1, 0, TC)
                    down(e, par, 1)
                pairs(q, lambda e, par: body(e, par, is_int(e) and e == E - 1))

            @block.scalar
            def _(q):
                def split_w(e, par):
                    q.wait_ge(s_w1, 16 * (e + 1))
                    wait(q, s_dn, TC * (e - 1))
                    q.activation(w1_hi[:, par, :, :], w1[:, :, :], ACT.Copy).then_inc(s_w1hi, 1)
                    q.wait_ge(s_w2, 16 * (e + 1))
                    q.activation(w2_hi[:, par, :, :], w2[:, :, :], ACT.Copy).then_inc(s_w2hi, 1)

                def split_x(e):
                    for c in range(TC):
                        q.wait_ge(s_xT, TC * e + c + 1)
                        if c == 0:
                            wait(q, s_up, 2 * FC * e)
                        q.activation(xT_hi[:, :, c * P:(c + 1) * P],
                                     ps[:, X_BANK + bank_of(e, c), 0:D].rearrange("p (k t) -> p k t", k=KC),
                                     ACT.Copy).then_inc(s_xThi, 1)

                def hidden(e, h):
                    cn = HALVES[h][1]
                    for m in range(FC):
                        q.wait_ge(s_up, (2 * e + h) * FC + m + 1)
                        if m == 0:
                            wait(q, s_dn, TC * (e - 1) + sum(HALVES[h]))
                        q.activation(h_hi[:, h, m, 0:cn * P], ps[:, UP_BANK + m % 4, 0:cn * P], ACT.Relu).then_inc(s_hhi, 1)

                split_w(0, 0)
                split_x(0)

                def body(e, par, last=False):
                    hidden(e, 0)
                    if not last:
                        split_w(e + 1, 1 - par)
                    hidden(e, 1)
                    if not last:
                        split_x(e + 1)
                pairs(q, lambda e, par: body(e, par, is_int(e) and e == E - 1))

            @block.vector
            def _(q):
                def split_w(e, par):
                    q.wait_ge(s_w1hi, e + 1)
                    q.tensor_tensor(w1_lo[:, par, :, :], w1[:, :, :], w1_hi[:, par, :, :].bitcast(F32),
                                    ALU.subtract).then_inc(s_w1lo, 1)

                def split_x(e):
                    for c in range(TC):
                        q.wait_ge(s_xThi, TC * e + c + 1)
                        q.tensor_tensor(xT_lo[:, :, c * P:(c + 1) * P],
                                        ps[:, X_BANK + bank_of(e, c), 0:D].rearrange("p (k t) -> p k t", k=KC),
                                        xT_hi[:, :, c * P:(c + 1) * P].bitcast(F32), ALU.subtract).then_inc(s_xTlo, 1)

                def hidden(e, h):
                    cn = HALVES[h][1]
                    for m in range(FC):
                        q.wait_ge(s_hhi, (2 * e + h) * FC + m + 1)
                        q.scalar_tensor_tensor(h_lo[:, h, m, 0:cn * P], ps[:, UP_BANK + m % 4, 0:cn * P], 0.0,
                                               h_hi[:, h, m, 0:cn * P].bitcast(F32), ALU.max,
                                               ALU.subtract).then_inc(s_hlo, 1)

                def outputs(e, par, h):
                    c0, cn = HALVES[h]
                    wait(q, s_st[h], 16 * e)
                    for c in range(cn):
                        q.wait_ge(s_dn, TC * e + c0 + c + 1)
                        if not is_int(e):
                            q.sem_inc(p.s_land, 1)
                        q.tensor_copy(y[:, h, c, :], ps[:, Y_BANK + (c0 + c + par) % 2, 0:D]).then_inc(s_y, 1)

                split_w(0, 0)
                split_x(0)

                def body(e, par, last=False):
                    hidden(e, 0)
                    if not last:
                        split_w(e + 1, 1 - par)
                    hidden(e, 1)
                    outputs(e, par, 0)
                    if not last:
                        split_x(e + 1)
                    outputs(e, par, 1)
                pairs(q, lambda e, par: body(e, par, is_int(e) and e == E - 1))

            @block.gpsimd
            def _(q):
                def split_w(e, par):
                    q.wait_ge(s_w2hi, e + 1)
                    q.tensor_tensor(w2_lo[:, par, :, :], w2[:, :, :], w2_hi[:, par, :, :].bitcast(F32),
                                    ALU.subtract).then_inc(s_w2lo, 1)
                pairs(q, split_w)


def experts_top2(p, ins):
    nc, ps = p.nc, p.psum
    FC, TC = F1 // P, T1 // P
    n = "E1_"
    with ExitStack() as st:
        wg, wv = (p.sb(st, n + x, [P, 2, KC, F1]) for x in ("wg", "wv"))
        w2 = p.sb(st, n + "w2", [P, 2, FC, D])
        wg_hi, wg_lo, wv_hi, wv_lo = (p.sb(st, n + x, [P, 2, KC, F1], F32R) for x in ("wg_hi", "wg_lo", "wv_hi", "wv_lo"))
        w2_hi, w2_lo = (p.sb(st, n + x, [P, 2, FC, D], F32R) for x in ("w2_hi", "w2_lo"))
        xin = p.sb(st, n + "xin", [P, 2, TC, DW])
        xT_hi, xT_lo = (p.sb(st, n + x, [P, KC, T1], F32R) for x in ("xT_hi", "xT_lo"))
        sg = p.sb(st, n + "sg", [P, FC, T1])
        hf = p.sb(st, n + "hf", [P, FC, T1])
        h_hi, h_lo = (p.sb(st, n + x, [P, 2, FC, T1], F32R) for x in ("h_hi", "h_lo"))
        y = p.sb(st, n + "y", [P, 2, TC, D])
        wt, dest = p.sb(st, n + "wt", [P, 2, TC, 1]), p.sb(st, n + "dest", [P, 2, TC, 1], I32)
        ma, mb = (p.sb(st, n + x, [P, TC, 1]) for x in ("ma", "mb"))
        spare = p.sb(st, n + "spare", [P, TC, 1])
        shift = p.sb(st, n + "shift", [P, TC, 1])
        tiles = p.sb(st, n + "tiles", [P, 1, E])
        tiles_a = p.sb(st, n + "tiles_a", [P, 1, E])
        tiles_i = p.sb(st, n + "tiles_i", [P, 1, E], I32)
        cmp = p.sb(st, n + "cmp", [P, NT1, E])
        num = p.sb(st, n + "num", [P, NT1, 1])
        num_i = p.sb(st, n + "num_i", [P, NT1], I32)
        own = p.sb(st, n + "own", [P, NT1, 1])
        base = p.sb(st, n + "base", [P, 1, E])
        first = p.sb(st, n + "first", [P, NT1, 1])
        ra, rb = (p.sb(st, n + x, [P, NT1, 1]) for x in ("ra", "rb"))
        tab = p.sb(st, n + "tab", [P, 2, NT1], I32)
        tail_i = p.sb(st, n + "tail_i", [P, E], I32)
        zero = p.sb(st, n + "zero", [P, TC * DW])
        S = lambda name: p.sem(n + name)
        s_z, s_tb, s_tab, s_tail = S("zeros"), S("table_steps"), S("table"), S("tails_zeroed")
        s_w, s_w2, s_x = ([S(f"{x}_loaded{j}") for j in range(2)] for x in ("w1", "w2", "x"))
        s_w2hi, s_w2lo = S("w2_hi"), S("w2_lo")
        s_whi, s_wlo, s_xT, s_xThi, s_xTlo = S("w_hi"), S("w_lo"), S("xT"), S("xT_hi"), S("xT_lo")
        s_up, s_sg, s_hf, s_hhi, s_hlo, s_dn, s_y = (S(x) for x in ("up", "silu", "h", "h_hi", "h_lo", "down", "y_scaled"))
        s_mt, s_wt, s_add = S("meta_steps"), S("weights_of_rows"), S("rows_added")
        UP_BANK, X_BANK, Y_BANK = 0, 4, 6
        d1 = p.d1
        wd = [ins[x].rearrange("e (c p) f -> p e c f", p=P) for x in ("w11", "w12")]
        w2_d = ins["w22"].rearrange("e (m p) d -> p e m d", p=P)

        def nth(i):
            return (i + 2) // 2 if is_int(i) else (i + 2) >> 1

        def tiles_loop(eng, body):
            body(0, 0, False)
            body(1, 1, False)
            with eng.Fori(1, NT1 // 2) as j:
                body(2 * j, 0, False)
                body(2 * j + 1, 1, False)
            body(NT1 - 1, 0, True)
        assert NT1 % 2 == 1

        def land(eng, i):
            if not is_int(i):
                eng.sem_inc(p.s_land, 1)

        with nc.Block() as block:
            @block.sync
            def _(q):
                def expert(i):
                    return q.value_load(tab[0:1, 1, i:i + 1] if is_int(i) else tab[0:1, 1, bass.ds(i, 1)], min_val=0, max_val=E - 1)

                def load_w(i, par):
                    e = expert(i)
                    wait(q, s_wlo, 2 * (i - 1))
                    land(q, i)
                    q.dma_start(wg[:, par, :, :], wd[0][:, e, :, :]).then_inc(s_w[par], 16)
                    q.dma_start(wv[:, par, :, :], wd[1][:, e, :, :]).then_inc(s_w[par], 16)

                def load_w2(i, par):
                    e = expert(i)
                    wait(q, s_w2lo, i - 1)
                    land(q, i)
                    q.dma_start(w2[:, par, :, :], w2_d[:, e, :, :]).then_inc(s_w2[par], 16)

                def load_x(i, par):
                    r = q.value_load(tab[0:1, 0, i:i + 1] if is_int(i) else tab[0:1, 0, bass.ds(i, 1)], min_val=0, max_val=IDLE_ROW)
                    wait(q, s_wt, i - 1)
                    wait(q, s_xT, i - 1)
                    land(q, i)
                    q.dma_start(xin[:, par, :, :],
                                d1[bass.ds(r, T1), :].rearrange("(c p) d -> p c d", p=P)).then_inc(s_x[par], 16)
                q.wait_ge(s_tab, 1)
                q.wait_ge(s_z, 1)
                for e in range(E):
                    r = q.value_load(tail_i[0:1, e:e + 1], min_val=0, max_val=IDLE_ROW - T1)
                    q.dma_start(d1[bass.ds(r, T1), :].rearrange("(p c) d -> p (c d)", p=P), zero[:, :]).then_inc(s_tail, 16)
                q.wait_ge(s_tab, 2)
                load_w(0, 0)
                load_w2(0, 0)
                q.wait_ge(s_tail, 16 * E)
                load_x(0, 0)

                def body(i, par, last):
                    if not last:
                        load_w(i + 1, 1 - par)
                        load_x(i + 1, 1 - par)
                        load_w2(i + 1, 1 - par)
                tiles_loop(q, body)

            @block.tensor
            def _(q):
                def transposes(i, par):
                    q.wait_ge(s_x[par], 16 * nth(i))
                    wait(q, s_xTlo, i)
                    for c in range(TC):
                        for kc in range(KC):
                            mm = q.transpose(ps[:, X_BANK + kc, c * P:(c + 1) * P],
                                             xin[:, par, c, kc * P:(kc + 1) * P], p.ident[:, :])
                    mm.then_inc(s_xT, 1)

                def down(i, par):
                    wait(q, s_w2lo, i + 1)
                    wait(q, s_hlo, (i + 1) * FC)
                    for c in range(TC):
                        wait(q, s_y, TC * i + c - 1)
                        k = 0
                        for m in range(FC):
                            for a, w in ((h_hi, w2_hi), (h_lo, w2_hi), (h_hi, w2_lo)):
                                mm = q.matmul(ps[:, Y_BANK + c, 0:D], a[:, par, m, c * P:(c + 1) * P], w[:, par, m, :],
                                              start=(k == 0), stop=(k == 3 * FC - 1))
                                k += 1
                        mm.then_inc(s_dn, 1)

                def body(i, par, last):
                    q.wait_ge(s_xTlo, i + 1)
                    q.wait_ge(s_wlo, 2 * i + 2)
                    for m in range(FC):
                        wait(q, s_hf, i * FC + m - 3)
                        for half, (hi, lo) in enumerate(((wg_hi, wg_lo), (wv_hi, wv_lo))):
                            bank = ps[:, UP_BANK + m, half * T1:(half + 1) * T1]
                            k = 0
                            for c in range(KC):
                                for a, x in ((hi, xT_hi), (hi, xT_lo), (lo, xT_hi)):
                                    mm = q.matmul(bank, a[:, par, c, m * P:(m + 1) * P], x[:, c, :],
                                                  start=(k == 0), stop=(k == 3 * KC - 1))
                                    k += 1
                        mm.then_inc(s_up, 1)
                    if not last:
                        transposes(i + 1, 1 - par)
                    if not is_int(i) or i > 0:
                        down(i - 1, 1 - par)
                    if last:
                        down(i, par)
                transposes(0, 0)
                tiles_loop(q, body)

            @block.scalar
            def _(q):
                def split_w(i, par, j):
                    if j == 0:
                        q.wait_ge(s_w[par], 32 * nth(i))
                        wait(q, s_up, FC * (i - 1))
                    hi, w = ((wg_hi, wg), (wv_hi, wv))[j]
                    q.activation(hi[:, par, :, :], w[:, par, :, :], ACT.Copy).then_inc(s_whi, 1)

                def split_w2(i, par):
                    q.wait_ge(s_w2[par], 16 * nth(i))
                    wait(q, s_dn, TC * (i - 1))
                    q.activation(w2_hi[:, par, :, :], w2[:, par, :, :], ACT.Copy).then_inc(s_w2hi, 1)

                def split_x(i, par):
                    q.wait_ge(s_xT, i + 1)
                    q.activation(xT_hi[:, :, :], ps[:, X_BANK:X_BANK + KC, 0:T1], ACT.Copy).then_inc(s_xThi, 1)

                def hidden_hi(i, par, m):
                    q.wait_ge(s_hf, i * FC + m + 1)
                    if m == 0:
                        wait(q, s_dn, TC * (i - 1))
                    q.activation(h_hi[:, par, m, :], hf[:, m, :], ACT.Copy).then_inc(s_hhi, 1)

                def body(i, par, last):
                    for m in range(FC):
                        q.wait_ge(s_up, i * FC + m + 1)
                        wait(q, s_hf, (i - 1) * FC + m + 1)
                        q.activation(sg[:, m, :], ps[:, UP_BANK + m, 0:T1], ACT.Silu).then_inc(s_sg, 1)
                        if m < 2 and not last:
                            split_w(i + 1, 1 - par, m)
                        if m == 2:
                            split_w2(i, par)
                        if 0 < m < 3:
                            hidden_hi(i, par, m - 1)
                    if not last:
                        split_x(i + 1, 1 - par)
                    for m in (2, 3):
                        hidden_hi(i, par, m)
                for j in range(2):
                    split_w(0, 0, j)
                split_x(0, 0)
                tiles_loop(q, body)

            @block.vector
            def _(q):
                q.tensor_copy(tail_i[:, :], p.next[:, 0, :]).then_inc(s_tab, 1)
                c = Chain(q, s_tb, 0, 28)
                c(q.scalar_tensor_tensor(tiles_a[:, 0, :], p.expert8[:, 0, :], -float(ROOM), p.next[:, 0, :],
                                         ALU.mult, ALU.add))
                c(q.tensor_scalar(tiles_a[:, 0, :], tiles_a[:, 0, :], float(T1 - 1), None, ALU.add))
                c(q.tensor_copy(tiles_i[:, 0, :], tiles_a[:, 0, :]))
                c(q.tensor_scalar(tiles_i[:, 0, :], tiles_i[:, 0, :], 8, None, ALU.arith_shift_right))
                c(q.tensor_copy(base[:, 0, :], tiles_i[:, 0, :]))
                c(q.tensor_copy(tiles[:, 0, 0:1], base[:, 0, 0:1]))
                for e in range(1, E):
                    c(q.tensor_tensor(tiles[:, 0, e:e + 1], tiles[:, 0, e - 1:e], base[:, 0, e:e + 1], ALU.add))
                c(q.tensor_tensor(base[:, 0, :], tiles[:, 0, :], base[:, 0, :], ALU.subtract))
                c(q.tensor_scalar(base[:, 0, :], base[:, 0, :], -float(T1), None, ALU.mult))
                c(q.scalar_tensor_tensor(base[:, 0, :], p.expert8[:, 0, :], float(ROOM), base[:, 0, :], ALU.mult, ALU.add))
                q.wait_ge(s_z, 2)
                c(q.tensor_copy(num[:, :, 0], num_i[:, :]))
                c(q.tensor_tensor(cmp[:, :, :], num[:, :, :].to_broadcast([P, NT1, E]),
                                  tiles[:, :, :].to_broadcast([P, NT1, E]), ALU.is_ge))
                c(q.tensor_reduce(own[:, :, 0], cmp[:, :, :], AX.X, ALU.add))
                c(q.tensor_tensor(cmp[:, :, :], own[:, :, :].to_broadcast([P, NT1, E]),
                                  p.expert8[:, :, :].to_broadcast([P, NT1, E]), ALU.is_equal))
                c(q.tensor_tensor(cmp[:, :, :], cmp[:, :, :], base[:, :, :].to_broadcast([P, NT1, E]), ALU.mult))
                c(q.tensor_reduce(first[:, :, 0], cmp[:, :, :], AX.X, ALU.add))
                c(q.scalar_tensor_tensor(first[:, :, 0], num[:, :, 0], float(T1), first[:, :, 0], ALU.mult, ALU.add))
                c(q.tensor_scalar(ra[:, :, :], own[:, :, :], float(E), None, ALU.is_equal))
                c(q.tensor_scalar(rb[:, :, :], first[:, :, :], -1.0, float(IDLE_ROW), ALU.mult, ALU.add))
                c(q.tensor_tensor(rb[:, :, :], rb[:, :, :], ra[:, :, :], ALU.mult))
                q.tensor_tensor(tab[:, 0, :], first[:, :, 0], rb[:, :, 0], ALU.add)
                q.tensor_scalar(tab[:, 1, :], own[:, :, 0], float(E - 1), None, ALU.min).then_inc(s_tab, 1)
                c(q.tensor_scalar(own[:, :, 0], own[:, :, 0], -1.0, float(E), ALU.mult, ALU.add))
                for r in range(TC):
                    q.tensor_scalar(spare[:, r, :], p.token[:, r:r + 1], float(TOK), None, ALU.add)
                    last = q.tensor_scalar(shift[:, r, :], p.token[:, r:r + 1], -1.0, float(T1), ALU.mult, ALU.add)
                c(last)
                c.end()

                def split_w(i, par, j):
                    hi, lo, w = ((wg_hi, wg_lo, wg), (wv_hi, wv_lo, wv))[j]
                    q.wait_ge(s_whi, 2 * i + j + 1)
                    q.tensor_tensor(lo[:, par, :, :], w[:, par, :, :], hi[:, par, :, :].bitcast(F32),
                                    ALU.subtract).then_inc(s_wlo, 1)

                def split_w2(i, par):
                    q.wait_ge(s_w2hi, i + 1)
                    q.tensor_tensor(w2_lo[:, par, :, :], w2[:, par, :, :], w2_hi[:, par, :, :].bitcast(F32),
                                    ALU.subtract).then_inc(s_w2lo, 1)

                def split_x(i, par):
                    q.wait_ge(s_xThi, i + 1)
                    q.tensor_tensor(xT_lo[:, :, :], ps[:, X_BANK:X_BANK + KC, 0:T1], xT_hi[:, :, :].bitcast(F32),
                                    ALU.subtract).then_inc(s_xTlo, 1)

                def meta(i, par):
                    q.wait_ge(s_x[par], 16 * nth(i))
                    wait(q, s_add, 16 * TC * (i - 1))
                    z = Chain(q, s_mt, i, 5)
                    m = lambda j: xin[:, par, :, D + j:D + j + 1]
                    own_i = own[:, i:i + 1, 0] if is_int(i) else own[:, bass.ds(i, 1), 0]
                    z(q.tensor_tensor(ma[:, :, :], m(0), m(1), ALU.subtract))
                    z(q.scalar_tensor_tensor(ma[:, :, 0], xin[:, par, :, D + 3], own_i, ma[:, :, 0], ALU.is_equal, ALU.mult))
                    z(q.tensor_tensor(wt[:, par, :, :], ma[:, :, :], m(1), ALU.add))
                    z(q.scalar_tensor_tensor(mb[:, :, 0], xin[:, par, :, D + 2], 0.0, shift[:, :, 0], ALU.is_lt, ALU.mult))
                    z(q.tensor_tensor(mb[:, :, :], mb[:, :, :], spare[:, :, :], ALU.add))
                    q.tensor_tensor(dest[:, par, :, :], m(2), mb[:, :, :], ALU.add).then_inc(s_wt, 1)
                    z.end()

                def outputs(i, par):
                    for c_ in range(TC):
                        wait(q, s_dn, TC * i + c_ + 1)
                        wait(q, s_wt, i + 1)
                        q.tensor_scalar(y[:, par, c_, :], ps[:, Y_BANK + c_, 0:D], wt[:, par, c_, :], None,
                                        ALU.mult).then_inc(s_y, 1)

                def body(i, par, last):
                    for m in range(FC):
                        q.wait_ge(s_sg, i * FC + m + 1)
                        wait(q, s_hlo, (i - 1) * FC + m + 1)
                        q.tensor_tensor(hf[:, m, :], ps[:, UP_BANK + m, T1:2 * T1], sg[:, m, :],
                                        ALU.mult).then_inc(s_hf, 1)
                        if m < 2 and not last:
                            split_w(i + 1, 1 - par, m)
                        if m == 2:
                            split_w2(i, par)
                    if not last:
                        split_x(i + 1, 1 - par)
                    meta(i, par)
                    if not is_int(i) or i > 0:
                        outputs(i - 1, 1 - par)
                    if last:
                        outputs(i, par)
                for j in range(2):
                    split_w(0, 0, j)
                split_x(0, 0)
                tiles_loop(q, body)

            @block.gpsimd
            def _(q):
                q.memset(zero[:, :], 0.0).then_inc(s_z, 1)
                q.iota(num_i[:, :], pattern=[[1, NT1]], base=0, channel_multiplier=0).then_inc(s_z, 1)

                def add(i, par):
                    for c in range(TC):
                        wait(q, s_y, TC * i + c + 1)
                        wait(q, s_add, 16 * (TC * i + c))
                        land(q, i)
                        q.indirect_dma_start(p.out[:, :], bass.IndirectOffsetOnAxis(ap=dest[:, par, c, :], axis=0),
                                             y[:, par, c, :], None, compute_op=ALU.add).then_inc(s_add, 16)

                def body(i, par, last):
                    for m in range(FC):
                        q.wait_ge(s_hhi, i * FC + m + 1)
                        q.tensor_tensor(h_lo[:, par, m, :], hf[:, m, :], h_hi[:, par, m, :].bitcast(F32),
                                        ALU.subtract).then_inc(s_hlo, 1)
                    if not is_int(i) or i > 0:
                        add(i - 1, 1 - par)
                    if last:
                        add(i, par)
                tiles_loop(q, body)
                q.wait_ge(s_add, 16 * TC * NT1)


def build(nc, ins, out):
    p = Program(nc)
    p.out = out
    p.d0 = nc.dram_tensor("rows0", [D0_ROWS, D], F32, kind="Internal").ap()
    p.d1 = nc.dram_tensor("rows1", [D1_ROWS, DW], F32, kind="Internal").ap()
    p.s_land = p.sem("landing")
    first = ExitStack()
    constants(p, first)
    for layer in range(2):
        with ExitStack() as st:
            mats = attention_setup(p, layer, ins, st)
            attention(p, layer, ins, mats, st)
        if layer == 0:
            first.close()
            p.phase()
            experts_capacity(p, ins)
            p.phase()
        else:
            p.phase()
            experts_top2(p, ins)
    p.keep.close()


def kernel(x, ctx_768, mask_BxS2_bk0, L0_xattn_W_q, L0_xattn_W_k, L0_xattn_W_v, L0_xattn_W_o, L0_xattn_b_o,
           L0_ffn_Wr, L0_ffn_W1, L0_ffn_W2, L1_xattn_w_q, L1_xattn_w_k, L1_xattn_w_v, L1_xattn_w_o,
           L1_xattn_b_o, L1_ffn_Wg, L1_ffn_W11, L1_ffn_W12, L1_ffn_W2):
    import concourse.bacc as bacc
    from concourse.bass_utils import run_bass_kernel_spmd as run

    a = lambda v: np.ascontiguousarray(np.asarray(v))
    arrays = {
        "x": a(x).reshape(TOK, D),
        "ctxT": a(a(ctx_768).reshape(B * KEYS, CTX).T),
        "mask": a(mask_BxS2_bk0).reshape(1, B * KEYS),
        "wqT0": a(a(L0_xattn_W_q).T), "wk0": a(L0_xattn_W_k), "wv0": a(L0_xattn_W_v), "wo0": a(L0_xattn_W_o),
        "bo0": a(L0_xattn_b_o).reshape(1, D),
        "wr0": a(L0_ffn_Wr), "w1": a(L0_ffn_W1), "w2": a(L0_ffn_W2),
        "wqT1": a(a(L1_xattn_w_q).T), "wk1": a(L1_xattn_w_k), "wv1": a(L1_xattn_w_v), "wo1": a(L1_xattn_w_o),
        "bo1": a(L1_xattn_b_o).reshape(1, D),
        "wr1": a(L1_ffn_Wg), "w11": a(L1_ffn_W11), "w12": a(L1_ffn_W12), "w22": a(L1_ffn_W2),
    }
    nc = bacc.Bacc("TRN2", target_bir_lowering=False, num_devices=1)
    ins = {name: nc.dram_tensor("in_" + name, v.shape, mybir.dt.from_np(v.dtype), kind="ExternalInput").ap()
           for name, v in arrays.items()}
    out = nc.dram_tensor("out", (TOK + T1, D), F32, kind="ExternalOutput").ap()
    build(nc, ins, out)
    r = run(nc, [{"in_" + name: v for name, v in arrays.items()}], core_ids=[0])
    return r.results[0]["out"][0:TOK].reshape(B, SEQ, D)
```

```python
from contextlib import ExitStack

import numpy as np
import concourse.bass as bass
import concourse.mybir as mybir
from concourse.alu_op_type import AluOpType as ALU

F32 = mybir.dt.float32
F32R = mybir.dt.float32r
BF16 = mybir.dt.bfloat16
I32 = mybir.dt.int32
U8 = mybir.dt.uint8
ACT = mybir.ActivationFunctionType
AX = mybir.AxisListType

P = 128
B, SEQ, D = 4, 1024, 256
TOK = B * SEQ
NT = TOK // P
KC = D // P
KEYS, CTX, DH = 64, 192, 64
CP = CTX // 2
E = 8
EPS = 1e-5
BIG = -3.3895313892515355e38
G = 4
CAP = int(1.25 * TOK / E)
F0 = 1024
D0_ROWS = E * CAP + TOK
F1 = 512
T1 = 256
ROOM = TOK + T1
IDLE_ROW = E * ROOM
D1_ROWS = IDLE_ROW + T1
NT1 = (2 * TOK + E * (T1 - 1)) // T1
META = 4
DW = D + META


def is_int(v):
    return isinstance(v, (int, np.integer))


def wait(eng, sem, value):
    if not is_int(value) or value > 0:
        eng.wait_ge(sem, value)


class Chain:

    def __init__(self, eng, sem, round_, n):
        self.eng, self.sem, self.base, self.n, self.j = eng, sem, round_ * n, n, 0

    def __call__(self, ins):
        self.j += 1
        ins.then_inc(self.sem, 1)
        self.eng.wait_ge(self.sem, self.base + self.j)

    def end(self):
        assert self.j == self.n, (self.j, self.n)


class Steps:

    def __init__(self, eng, sem, round_, n, steps):
        self.eng, self.sem, self.base, self.steps, self.j = eng, sem, round_ * n, list(steps), 0

    def add_wait(self, sem, value):
        self.steps.insert(0, (sem, value))

    def more(self, n, hold=None):
        while n > 0 and self.steps:
            if isinstance(self.steps[0], tuple) and self.steps[0][0] is hold:
                return
            s = self.steps.pop(0)
            if isinstance(s, tuple):
                wait(self.eng, *s)
                continue
            if self.j:
                self.eng.wait_ge(self.sem, self.base + self.j)
            s().then_inc(self.sem, 1)
            self.j += 1
            n -= 1


class Program:
    def __init__(self, nc):
        self.nc = nc
        self.keep = ExitStack()
        self.sems = []
        self.phases = 0

    def sb(self, stack, name, shape, dt=F32):
        return stack.enter_context(self.nc.sbuf_tensor(name, shape, dt))

    def sem(self, name):
        s = self.nc.alloc_semaphore(name=name)
        self.sems.append(s)
        return s

    def phase(self):
        self.nc.clear_and_free_semaphores(self.sems)
        self.sems = []
        self.nc.all_engine_barrier()
        self.phases += 1
        self.s_land = self.sem(f"landing{self.phases}")


def constants(p, first):
    nc, k = p.nc, p.keep
    p.x = p.sb(k, "x", [P, NT, D])
    p.ident = p.sb(k, "ident", [P, P])
    p.first_head = p.sb(k, "first_head", [1, P], F32R)
    p.ones_b = p.sb(k, "ones_b", [P, P], BF16)
    p.below = p.sb(k, "below", [P, P], BF16)
    p.half = p.sb(k, "half", [P, 1])
    p.eps = p.sb(k, "eps", [P, 2])
    p.first8 = p.sb(k, "first8", [P, 1, E])
    p.expert8 = p.sb(k, "expert8", [P, 1, E])
    p.token = p.sb(k, "token", [P, NT])
    p.iota_i = p.sb(k, "iota_i", [P, NT], I32)
    p.tab = p.sb(k, "tab", [P, 2, NT1], I32)
    p.own = p.sb(k, "own", [P, NT1, 1])
    p.spare = p.sb(k, "spare", [P, T1 // P, 1])
    p.shift = p.sb(k, "shift", [P, T1 // P, 1])
    p.factor0 = p.sb(k, "factor0", [P, NT])
    p.row0 = p.sb(k, "row0", [P, NT], I32)
    p.next = p.sb(k, "next_row", [P, 1, E])
    p.psum = k.enter_context(nc.psum_tensor("psum", [P, 8, 512], F32))
    p.zero = p.sb(first, "zero", [P, CAP // P * D])
    p.w1 = p.sb(first, "w1", [P, KC, F0])
    p.w2 = p.sb(first, "w2", [P, F0 // P, D])
    p.s_x, p.s_zero, p.s_zeroed = p.sem("x_loaded"), p.sem("zero_memset"), p.sem("zero_fill")
    s_c, s_i = p.sem("const_memset"), p.sem("const_select")
    with nc.Block() as block:
        @block.gpsimd
        def _(e):
            e.memset(p.ident[:, :], 0.0).then_inc(s_c, 1)
            e.memset(p.ones_b[:, :], 1.0).then_inc(s_c, 1)
            e.memset(p.half[:, :], -0.5)
            e.memset(p.eps[:, 0:1], 0.0)
            e.memset(p.eps[:, 1:2], EPS)
            e.wait_ge(s_c, 2)
            e.affine_select(out=p.ident[:, :], in_=p.ident[:, :], compare_op=ALU.not_equal, fill=1.0,
                            base=0, pattern=[[-1, P]], channel_multiplier=1).then_inc(s_i, 1)
            e.affine_select(out=p.below[:, :], in_=p.ones_b[:, :], compare_op=ALU.is_gt, fill=0.0,
                            base=0, pattern=[[1, P]], channel_multiplier=-1).then_inc(s_i, 1)
            e.iota(p.iota_i[:, :], pattern=[[P, NT]], base=0, channel_multiplier=1).then_inc(s_i, 1)

        @block.vector
        def _(e):
            e.memset(p.zero[:, :], 0.0).then_inc(p.s_zero, 1)
            for j in range(E):
                e.memset(p.expert8[:, :, j:j + 1], float(j))
                e.memset(p.first8[:, :, j:j + 1], float(E - j))
            e.wait_ge(s_i, 3)
            e.tensor_copy(p.token[:, :], p.iota_i[:, :])
            e.tensor_copy(p.first_head[:, 0:KEYS], p.ones_b[0:1, 0:KEYS])
            e.tensor_scalar(p.first_head[:, KEYS:P], p.ones_b[0:1, KEYS:P], 0.0, None, ALU.mult)


def first_loads(p, e, ins):
    for q in range(4):
        t = slice(q * NT // 4, (q + 1) * NT // 4)
        e.dma_start(p.x[:, t, :], ins["x"].rearrange("(t p) d -> p t d", p=P)[:, t, :]).then_inc(p.s_x, 16)
    e.wait_ge(p.s_zero, 1)
    for q in range(E):
        e.dma_start(p.d0[q * CAP:(q + 1) * CAP, :].rearrange("(p r) d -> p (r d)", p=P),
                    p.zero[:, :]).then_inc(p.s_zeroed, 16)
        r0, n = E * CAP + q * SEQ // 2, SEQ // 2
        e.dma_start(p.d0[r0:r0 + n, :].rearrange("(p r) d -> p (r d)", p=P),
                    p.zero[:, 0:n // P * D]).then_inc(p.s_zeroed, 16)
    e.dma_start(p.d1[IDLE_ROW:IDLE_ROW + T1, :].rearrange("(p r) d -> p (r d)", p=P),
                p.zero[:, 0:T1 // P * DW]).then_inc(p.s_zeroed, 16)
    e.dma_start(p.out[TOK:TOK + T1, :].rearrange("(p r) d -> p (r d)", p=P),
                p.zero[:, 0:T1 // P * D]).then_inc(p.s_zeroed, 16)


ZEROED = 16 * (2 * E + 2)


def attention_setup(p, layer, ins, st):
    nc = p.nc
    H = 8 if layer == 0 else 16
    PR, W, INNER = H // 2, H * KEYS, H * DH
    NB = W // 512
    n = f"L{layer}_"
    wr = p.sb(st, n + "wr", [P, KC, E])
    m_hi = p.sb(st, n + "m_hi", [P, B, KC, W], F32R)
    m_lo = p.sb(st, n + "m_lo", [P, B, KC, W], F32R)
    masked = p.sb(st, n + "masked", [1, B, W], BF16) if layer == 0 else None
    with ExitStack() as tmp:
        with ExitStack() as early:
            ctxT = p.sb(early, n + "ctxT", [CP, 2, B * KEYS])
            wk = p.sb(early, n + "wk", [CP, 2, INNER])
            wv = p.sb(early, n + "wv", [CP, 2, INNER])
            wqT = p.sb(early, n + "wqT", [P, PR, D])
        n_hi = p.sb(st, n + "n_hi", [P, B, PR, D], F32R)
        n_lo = p.sb(st, n + "n_lo", [P, B, PR, D], F32R)
        kd = p.sb(tmp, n + "kd", [P, PR, B, P])
        vd = p.sb(tmp, n + "vd", [P, PR, B, P])
        wo = p.sb(tmp, n + "wo", [P, PR, D])
        bo = p.sb(tmp, n + "bo", [1, D])
        bo_hi, bo_lo = (p.sb(tmp, n + x, [1, D], F32R) for x in ("bo_hi", "bo_lo"))
        if layer == 0:
            keep_u = p.sb(tmp, n + "keep_u", [P, B * KEYS], U8)
            keep = p.sb(tmp, n + "keep", [P, B, 1, KEYS])
        s_w, s_wo, s_zero, s_kv, s_kvc = (p.sem(n + x) for x in ("ctx_wk_loaded", "wo_loaded", "kd_zero", "kv", "kv_copied"))
        s_m, s_mhi, s_mlo = (p.sem(n + x) for x in ("m", "m_hi", "m_lo"))
        s_n, s_nhi, s_nlo, s_keep = (p.sem(n + x) for x in ("n", "n_hi", "n_lo", "keep"))
        s_wv, s_wq = p.sem(n + "wv_loaded"), p.sem(n + "wq_loaded")
        s_bo, s_wr, s_keep_u, s_bohi = (p.sem(n + x) for x in ("bo_loaded", "wr_loaded", "mask_loaded", "bo_hi"))
        ps = p.psum
        RING_M = 4 // NB

        def m_ps(j):
            return ps[:, j % RING_M * NB:(j % RING_M + 1) * NB, :].rearrange("p a b -> p (a b)")

        with nc.Block() as block:
            @block.sync
            def _(e):
                if layer == 0:
                    e.dma_start(keep_u[:, :], ins["mask"].to_broadcast([P, B * KEYS])).then_inc(s_keep_u, 16)
                e.dma_start(ctxT[:, :, :], ins["ctxT"].rearrange("(c p) k -> p c k", p=CP)).then_inc(s_w, 16)
                e.dma_start(wk[:, :, :], ins[f"wk{layer}"].rearrange("(c p) n -> p c n", p=CP)).then_inc(s_w, 16)
                e.dma_start(wv[:, :, :], ins[f"wv{layer}"].rearrange("(c p) n -> p c n", p=CP)).then_inc(s_wv, 16)
                e.dma_start(wqT[:, :, :], ins[f"wqT{layer}"].rearrange("(r p) d -> p r d", p=P)).then_inc(s_wq, 16)
                e.dma_start(wo[:, :, :], ins[f"wo{layer}"].rearrange("(r p) d -> p r d", p=P)).then_inc(s_wo, 16)
                e.dma_start(bo[:, :], ins[f"bo{layer}"]).then_inc(s_bo, 16)
                e.dma_start(wr[:, :, :], ins[f"wr{layer}"].rearrange("(c p) e -> p c e", p=P)).then_inc(s_wr, 16)
                if layer == 0:
                    first_loads(p, e, ins)

            @block.gpsimd
            def _(e):
                e.memset(vd[:, :, :, :], 0.0).then_inc(s_zero, 1)

            @block.tensor
            def _(e):
                e.wait_ge(s_w, 32)
                for j in range(2 * PR):
                    if j == PR:
                        e.wait_ge(s_wv, 16)
                    w, r = (wk, j) if j < PR else (wv, j - PR)
                    wait(e, s_kvc, j - 3)
                    for c in range(2):
                        mm = e.matmul(ps[:, j % 4, 0:B * KEYS], w[:, c, r * P:(r + 1) * P], ctxT[:, c, :],
                                      start=(c == 0), stop=(c == 1))
                    mm.then_inc(s_kv, 1)
                e.wait_ge(s_kvc, 2 * PR)
                e.wait_ge(s_wq, 16)
                for b in range(B):
                    for c in range(KC):
                        j = b * KC + c
                        wait(e, s_mlo, j - RING_M + 1)
                        for r in range(PR):
                            mm = e.matmul(ps[:, j % RING_M * NB + r // 4, (r % 4) * P:(r % 4 + 1) * P],
                                          wqT[:, r, c * P:(c + 1) * P], kd[:, r, b, :], start=True, stop=True)
                        mm.then_inc(s_m, 1)
                e.wait_ge(s_wo, 16)
                e.wait_ge(s_bohi, 2)
                for b in range(B):
                    for r in range(PR):
                        e.wait_ge(s_nlo, b * PR + r + 1)
                        o = ps[:, 4 + r % 4, 0:D]
                        mm = e.matmul(o, vd[:, r, b, :], wo[:, r, :], start=True, stop=(r > 0))
                        if r == 0:
                            e.matmul(o, p.first_head[:, :], bo_hi[:, :], start=False, stop=False)
                            mm = e.matmul(o, p.first_head[:, :], bo_lo[:, :], start=False, stop=True)
                        mm.then_inc(s_n, 1)
                e.wait_ge(s_wr, 16)

            @block.scalar
            def _(e):
                e.sem_inc(s_nlo, 4)
                for j in range(B * KC):
                    e.wait_ge(s_m, j + 1)
                    e.activation(m_hi[:, j // KC, j % KC, :], m_ps(j), ACT.Copy).then_inc(s_mhi, 1)
                with e.Fori(0, B) as b:
                    for r in range(PR):
                        e.wait_ge(s_n, b * PR + r + 1)
                        e.sem_inc(p.s_land, 1)
                        e.activation(n_hi[:, b, r, :], ps[:, 4 + r % 4, 0:D], ACT.Copy).then_inc(s_nhi, 1)

            @block.vector
            def _(e):
                e.memset(kd[:, :, :, :], 0.0).then_inc(s_zero, 1)
                for j in range(E):
                    e.memset(p.next[:, :, j:j + 1], float(j * (CAP if layer == 0 else ROOM)))
                if layer == 0:
                    e.wait_ge(s_keep_u, 16)
                    e.tensor_copy(keep[:, :, 0, :], keep_u[:, :].rearrange("p (b k) -> p b k", b=B)).then_inc(s_keep, 1)
                    e.wait_ge(s_keep, 1)
                e.wait_ge(s_zero, 2)
                for j in range(2 * PR):
                    d, r = (kd, j) if j < PR else (vd, j - PR)
                    e.wait_ge(s_kv, j + 1)
                    for h in range(2):
                        q = slice(h * DH, (h + 1) * DH)
                        to, kv = d[q, r, :, h * KEYS:(h + 1) * KEYS], ps[q, j % 4, 0:B * KEYS].rearrange("p (b k) -> p b k", b=B)
                        if j >= PR:
                            cp = e.tensor_copy(to, kv)
                        elif layer == 0:
                            cp = e.scalar_tensor_tensor(to, kv, DH ** -0.5, keep[q, :, 0, :], ALU.mult, ALU.mult)
                        else:
                            cp = e.tensor_scalar(to, kv, DH ** -0.5, None, ALU.mult)
                    cp.then_inc(s_kvc, 1)
                if layer == 0:
                    for b in range(B):
                        e.tensor_scalar(masked[:, b, :].rearrange("p (h k) -> p h k", h=H),
                                        keep[0:1, b, :, :].to_broadcast([1, H, KEYS]),
                                        -BIG, BIG, ALU.mult, ALU.add)
                e.wait_ge(s_bo, 16)
                e.tensor_copy(bo_hi[:, :], bo[:, :]).then_inc(s_bohi, 1)
                e.wait_ge(s_bohi, 1)
                e.tensor_tensor(bo_lo[:, :], bo[:, :], bo_hi[:, :].bitcast(F32), ALU.subtract).then_inc(s_bohi, 1)
                for j in range(B * KC):
                    e.wait_ge(s_mhi, j + 1)
                    e.tensor_tensor(m_lo[:, j // KC, j % KC, :], m_ps(j), m_hi[:, j // KC, j % KC, :].bitcast(F32),
                                    ALU.subtract).then_inc(s_mlo, 1)
                with e.Fori(0, B) as b:
                    for r in range(PR):
                        e.wait_ge(s_nhi, b * PR + r + 1)
                        e.tensor_tensor(n_lo[:, b, r, :], ps[:, 4 + r % 4, 0:D], n_hi[:, b, r, :].bitcast(F32),
                                        ALU.subtract).then_inc(s_nlo, 1)
    return m_hi, m_lo, n_hi, n_lo, masked, wr


def attention(p, layer, ins, mats, st):
    nc, ps = p.nc, p.psum
    m_hi, m_lo, n_hi, n_lo, masked, wr = mats
    H = 8 if layer == 0 else 16
    CH = 1 if layer == 0 else 2
    RA = 7 if layer == 0 else 13
    NR = 22 if layer == 0 else 30
    PR, W = H // 2, H * KEYS
    NB = W // 512
    TC = T1 // P
    n = f"L{layer}_"
    xn = p.sb(st, n + "xn", [P, 2, D])
    xT_hi = p.sb(st, n + "xT_hi", [P, 2, KC, P], F32R)
    xT_lo = p.sb(st, n + "xT_lo", [P, 2, KC, P], F32R)
    prob = p.sb(st, n + "prob", [P, 2, W])
    pT_hi = p.sb(st, n + "pT_hi", [P, PR, P], F32R)
    pT_lo = p.sb(st, n + "pT_lo", [P, PR, P], F32R)
    xf = p.sb(st, n + "xf", [P, 2, D])
    xfT = p.sb(st, n + "xfT", [P, KC, P])
    stage = p.sb(st, n + "stage", [P, G, DW])
    tails = p.sb(st, n + "tails", [P, 2 * G, META])
    rowf = p.sb(st, n + "rowf", [P, 2 * G, CH])
    row = p.sb(st, n + "row", [P, G, CH], I32)
    nmx, sm, rc = (p.sb(st, n + x, [P, 2, H, 1]) for x in ("neg_max", "sum", "rcp"))
    stats = p.sb(st, n + "stats", [P, 2, 6])
    mv1 = p.sb(st, n + "mv1", [P, G, 2])
    mv2 = p.sb(st, n + "mv2", [P, G, 2])
    mv = p.sb(st, n + "mv", [P, NT, 2])
    rs1 = p.sb(st, n + "rs1", [P, G])
    rs2 = p.sb(st, n + "rs2", [P, NT])
    nb2 = p.sb(st, n + "nb2", [P, NT])
    lg = p.sb(st, n + "lg", [P, G, E])
    sh, sh2, ex, a1, oh1, a2, oh2, pos, c1, c2 = (p.sb(st, n + x, [P, G, E]) for x in
                                                  ("sh", "sh2", "ex", "a1", "oh1", "a2", "oh2", "pos", "c1", "c2"))
    oh_b = p.sb(st, n + "oh_b", [P, G, E], BF16)
    ranks = p.sb(st, n + "ranks", [P, G + 1, E])
    f1, r1, r2, r3, r4, r5 = (p.sb(st, n + x, [P, G, 1]) for x in ("f1", "r1", "r2", "r3", "r4", "r5"))
    if layer == 1:
        tiles = p.sb(st, n + "tiles", [P, 1, E])
        tiles_a = p.sb(st, n + "tiles_a", [P, 1, E])
        tiles_i = p.sb(st, n + "tiles_i", [P, 1, E], I32)
        cmp = p.sb(st, n + "cmp", [P, NT1, E])
        num = p.sb(st, n + "num", [P, NT1, 1])
        num_i = p.sb(st, n + "num_i", [P, NT1], I32)
        base = p.sb(st, n + "base", [P, 1, E])
        first = p.sb(st, n + "first", [P, NT1, 1])
        ra, rb = (p.sb(st, n + x, [P, NT1, 1]) for x in ("ra", "rb"))
        tail_i = p.sb(st, n + "tail_i", [P, E], I32)
        zero = p.sb(st, n + "zero", [P, TC * DW])
        s_num, s_tb, s_tab, s_tail, s_zero = (p.sem(n + x) for x in ("number", "table_steps", "table", "tails_zeroed", "zero"))
        got = p.sb(st, n + "got", [P, G, D])
        gidx = p.sb(st, n + "gidx", [P, G], I32)

    S = lambda name: p.sem(n + name)
    s_gidx, s_got = S("gather_index"), [S(f"gathered{j}") for j in range(G)]
    s_cmb, s_st1, s_ch1, s_rs1, s_eps1 = S("combined"), S("stats1"), S("bn1"), S("rstd1"), S("eps1")
    s_xn, s_xT, s_xThi, s_xTlo = S("xn"), S("xT"), S("xT_hi"), S("xT_lo")
    s_sim, s_mx, s_exp, s_rcp, s_p = (S(x) for x in ("scores", "max", "exp", "reciprocal", "prob"))
    s_pT, s_pThi, s_pTlo, s_out, s_res = (S(x) for x in ("pT", "pT_hi", "pT_lo", "output", "residual"))
    s_ch2, s_st2, s_rs2, s_eps2, s_nb2, s_xf, s_xfT, s_xfTc, s_lgp, s_lg = (
        S(x) for x in ("bn2", "stats2", "rstd2", "eps2", "neg_mean2", "xf", "xfT", "xfT_copied", "logits", "logits_copied"))
    s_route, s_rexp, s_pos, s_posr = (S(x) for x in ("routing", "route_exp", "ranks", "ranks_copied"))
    s_stg, s_scat, s_store = S("staged"), [S(f"scattered{j}") for j in range(G)], S("x_stored")
    s_first = S("first_expert_loaded")

    S_BANK, T_BANK, O_BANK, X_BANK = 0, 4, 6, 7
    LOGITS = slice(0, E)
    RANKS = slice(256, 256 + (G + 1) * E)
    ok = lambda t: not is_int(t) or 0 <= t < NT
    okg = lambda g: not is_int(g) or 0 <= g < NT // G
    flat = lambda ap: ap.rearrange("p a b -> p (a b)")
    col = lambda ap, t: ap[:, t:t + 1] if is_int(t) else ap[:, bass.ds(t, 1)]

    def scores_ps(k):
        return flat(ps[:, S_BANK + (k % 2) * NB:S_BANK + (k % 2 + 1) * NB, :])

    def pT_ps():
        return flat(ps[:, T_BANK:T_BANK + NB, :])

    def cap(t):
        return min(t, NT) if is_int(t) else t

    def run(eng, body):
        for g in (-2, -1, 0, 1, 2):
            body(g)
        with eng.Fori(3, 6) as g:
            body(g)
        for g in (6, 7, 8, 9):
            body(g)

    def land(eng, t=None):
        if not is_int(t):
            eng.sem_inc(p.s_land, 1)

    with nc.Block() as block:
        @block.sync
        def _(e):
            if layer == 0:
                e.dma_start(p.w1[:, :, :], ins["w1"][0, :, :].rearrange("(c p) f -> p c f", p=P)).then_inc(s_first, 16)
                e.dma_start(p.w2[:, :, :], ins["w2"][0, :, :].rearrange("(m p) d -> p m d", p=P)).then_inc(s_first, 16)
                e.wait_ge(s_first, 32)
            if layer == 1:
                out_t = p.out[0:TOK, :].rearrange("(t p) d -> p t d", p=P)
                with e.Fori(0, NT) as t:
                    e.wait_ge(s_res, t + 1)
                    e.dma_start(out_t[:, t, :], p.x[:, t, :]).then_inc(s_store, 16)
                e.wait_ge(s_zero, 1)
                e.wait_ge(s_tab, 1)
                for j in range(E):
                    r = e.value_load(tail_i[0:1, j:j + 1], min_val=0, max_val=IDLE_ROW - T1)
                    e.dma_start(p.d1[bass.ds(r, T1), :].rearrange("(p c) d -> p (c d)", p=P), zero[:, :]).then_inc(s_tail, 16)
                e.wait_ge(s_tail, 16 * E)
                e.wait_ge(s_store, 16 * NT)

        def pe_body(e, g):
            if is_int(g):
                seq = (g // 2, (g + 1) // 2)
            else:
                seq = tuple(e.snap(v >> 1, min_val=0, max_val=B - 1) for v in (g, g + 1))
            for k in range(G):
                t = g * G + k
                if ok(t):
                    wait(e, s_p, t + 1)
                    wait(e, s_pTlo, t)
                    for r in range(PR):
                        mm = e.transpose(ps[:, T_BANK + r // 4, (r % 4) * P:(r % 4 + 1) * P],
                                         prob[:, k % 2, r * P:(r + 1) * P], p.ident[:, :])
                    mm.then_inc(s_pT, 1)
                if ok(t + 4) or ok(t - 2):
                    wait(e, s_xTlo, cap(t + 4))
                    wait(e, s_lg, cap(t - 2))
                if ok(t + 4):
                    wait(e, s_xn, t + 5)
                    for c in range(KC):
                        mm = e.transpose(ps[:, X_BANK, c * P:(c + 1) * P], xn[:, k % 2, c * P:(c + 1) * P],
                                         p.ident[:, :])
                    mm.then_inc(s_xT, 1)
                if ok(t - 2):
                    wait(e, s_xf, t - 1)
                    for c in range(KC):
                        mm = e.transpose(ps[:, X_BANK, 256 + c * P:256 + (c + 1) * P],
                                         xf[:, k % 2, c * P:(c + 1) * P], p.ident[:, :])
                    mm.then_inc(s_xfT, 1)
                if k == 3 and okg(g - 1):
                    wait(e, s_route, (g - 1) * NR + RA)
                    wait(e, s_res, cap(t))
                    rk = lambda j: ps[:, O_BANK, 256 + j * E:256 + G * E]
                    e.matmul(rk(0), p.below[:, :], flat(oh_b[:, :, :]), start=True, stop=False)
                    for j in range(1, G):
                        e.matmul(rk(j), p.ones_b[:, :], flat(oh_b[:, 0:G - j, :]), start=False, stop=(j == G - 1))
                    for j in range(G):
                        mm = e.matmul(ps[:, O_BANK, 256 + G * E:256 + (G + 1) * E], p.ones_b[:, :], oh_b[:, j, :],
                                      start=(j == 0), stop=(j == G - 1))
                    mm.then_inc(s_pos, 1)
                if ok(t + 3):
                    b = seq[(k + 3) // G]
                    wait(e, s_xTlo, t + 4)
                    wait(e, s_exp, t + 2)
                    land(e, t)
                    for q in range(NB):
                        bank = ps[:, S_BANK + ((k + 1) % 2) * NB + q, :]
                        if layer == 0:
                            e.matmul(bank, p.ones_b[0:1, :], masked[:, b, :], start=True, stop=False)
                        for c in range(KC):
                            for j, (a, m) in enumerate(((xT_hi, m_hi), (xT_lo, m_hi), (xT_hi, m_lo))):
                                mm = e.matmul(bank, a[:, (k + 1) % 2, c, :], m[:, b, c, q * 512:(q + 1) * 512],
                                              start=(layer == 1 and c == 0 and j == 0),
                                              stop=(c == KC - 1 and j == 2))
                    mm.then_inc(s_sim, 1)
                if ok(t):
                    b = seq[0]
                    wait(e, s_res, t)
                    if k == 3:
                        wait(e, s_posr, g)
                    o = ps[:, O_BANK, 0:D]
                    wait(e, s_pTlo, t + 1)
                    land(e, t)
                    for r in range(PR):
                        for j, (a, m) in enumerate(((pT_hi, n_hi), (pT_lo, n_hi), (pT_hi, n_lo))):
                            mm = e.matmul(o, a[:, r, :], m[:, b, r, :], start=(r == 0 and j == 0),
                                          stop=(r == PR - 1 and j == 2))
                    mm.then_inc(s_out, 1)
                if ok(t - 2):
                    wait(e, s_xfTc, t - 1)
                    wait(e, s_xTlo, cap(t + 5))
                    for c in range(KC):
                        mm = e.matmul(ps[:, X_BANK, LOGITS], xfT[:, c, :], wr[:, c, :], start=(c == 0), stop=(c == KC - 1))
                    mm.then_inc(s_lgp, 1)

        @block.tensor
        def _(e):
            run(e, lambda g: pe_body(e, g))

        def act_body(e, g):
            for k in range(G):
                t = g * G + k
                if ok(t):
                    wait(e, s_pT, t + 1)
                    e.activation(flat(pT_hi[:, :, :]), pT_ps(), ACT.Copy).then_inc(s_pThi, 1)
                if ok(t + 4):
                    wait(e, s_xT, t + 5)
                    wait(e, s_xfT, cap(t - 1))
                    e.activation(flat(xT_hi[:, k % 2, :, :]), ps[:, X_BANK, 0:D], ACT.Copy).then_inc(s_xThi, 1)
                if ok(t - 2):
                    wait(e, s_xfT, t - 1)
                    e.activation(flat(xfT[:, :, :]), ps[:, X_BANK, 256:512], ACT.Copy).then_inc(s_xfTc, 1)
                if k == 2 and okg(g - 1):
                    wait(e, s_route, (g - 1) * NR + 2)
                    e.activation(ex[:, :, :], sh[:, :, :], ACT.Exp).then_inc(s_rexp, 1)
                if ok(t - 8):
                    slot = (g % 2) * G + k
                    wait(e, s_route, (g - 1) * NR)
                    wait(e, s_nb2, t - 7)
                    wait(e, s_scat[k], 16 * CH * (g - 2))
                    land(e)
                    e.activation(stage[:, k, 0:D], p.x[:, t - 8, :], ACT.Identity, bias=col(nb2, t - 8),
                                 scale=col(rs2, t - 8))
                    if layer == 1:
                        e.activation(stage[:, k, D:DW], tails[:, slot, :], ACT.Copy)
                    e.activation(row[:, k, :], rowf[:, slot, :], ACT.Copy).then_inc(s_stg, 1)
                if ok(t + 2):
                    q = k % 2
                    wait(e, s_mx, t + 3)
                    wait(e, s_pT, t + 1)
                    for h in range(H):
                        last = e.activation(prob[:, q, h * KEYS:(h + 1) * KEYS], scores_ps(k)[:, h * KEYS:(h + 1) * KEYS],
                                            ACT.Exp, bias=nmx[:, q, h, :], accum_out=sm[:, q, h, :])
                    last.then_inc(s_exp, 1)

        @block.scalar
        def _(e):
            run(e, lambda g: act_body(e, g))

        def pool_body(e, g):
            for k in range(G):
                t = g * G + k
                if layer == 1 and ok(t + 8):
                    wait(e, s_cmb, t + 5)
                    land(e, t)
                    e.tensor_copy(gidx[:, k:k + 1], p.row0[:, bass.ds(t + 8, 1)]).then_inc(s_gidx, 1)
                    wait(e, s_gidx, t + 9)
                    land(e, t)
                    e.indirect_dma_start(got[:, k, :], None, p.d0[:, :],
                                         bass.IndirectOffsetOnAxis(ap=gidx[:, k:k + 1], axis=0)).then_inc(s_got[k], 16)
                if ok(t + 1):
                    q = (k + 1) % 2
                    wait(e, s_rcp, t + 2)
                    pr = prob[:, q, :].rearrange("p (h k) -> p h k", h=H)
                    e.tensor_tensor(pr, pr, rc[:, q, :, :].to_broadcast([P, H, KEYS]), ALU.mult).then_inc(s_p, 1)
                if layer == 0 and is_int(t) and t == 8:
                    e.wait_ge(p.s_zeroed, ZEROED)
                if ok(t - 8):
                    wait(e, s_stg, t - 7)
                    land(e, t)
                    for c in range(CH):
                        dst = p.d0 if layer == 0 else p.d1
                        width = D if layer == 0 else DW
                        e.indirect_dma_start(dst[:, :], bass.IndirectOffsetOnAxis(ap=row[:, k, c:c + 1], axis=0),
                                             stage[:, k, 0:width], None).then_inc(s_scat[k], 16)
                q = (k + 2) % G
                if ok(t + 6):
                    wait(e, s_st1, t + 7)
                    e.tensor_tensor(mv1[:, q, :], mv1[:, q, :], p.eps[:, :], ALU.add).then_inc(s_eps1, 1)
                if ok(t):
                    wait(e, s_st2, t + 1)
                    land(e, t)
                    e.tensor_tensor(mv[:, t, :], mv2[:, k, :], p.eps[:, :], ALU.add).then_inc(s_eps2, 1)
                if ok(t + 6):
                    wait(e, s_eps1, t + 7)
                    e.tensor_tensor(rs1[:, q:q + 1], mv1[:, q, 1:2], p.half[:, :], ALU.pow).then_inc(s_rs1, 1)
                if ok(t):
                    wait(e, s_eps2, t + 1)
                    land(e, t)
                    e.tensor_tensor(col(rs2, t), mv[:, t, 1:2], p.half[:, :], ALU.pow).then_inc(s_rs2, 1)

        @block.gpsimd
        def _(e):
            if layer == 1:
                e.iota(num_i[:, :], pattern=[[1, NT1]], base=0, channel_multiplier=0).then_inc(s_num, 1)
            run(e, lambda g: pool_body(e, g))
            for r in range(G):
                e.wait_ge(s_scat[r], 16 * CH * NT // G)

        def routing(e, gg, par):
            bc = [P, G, E]
            TT, TS, STT, RED = e.tensor_tensor, e.tensor_scalar, e.scalar_tensor_tensor, e.tensor_reduce
            slots = slice(par, par + G) if is_int(par) else bass.ds(par, G)
            gs = slice(gg * G, gg * G + G) if is_int(gg) else bass.ds(gg * G, G)
            tok = p.token[:, gs]
            steps = [lambda: RED(r1[:, :, 0], lg[:, :, :], AX.X, ALU.max),
                     lambda: TT(sh[:, :, :], lg[:, :, :], r1[:, :, :].to_broadcast(bc), ALU.subtract),
                     lambda: TS(a1[:, :, :], sh[:, :, :], 0.0, None, ALU.is_equal),
                     lambda: TT(a1[:, :, :], a1[:, :, :], p.first8[:, :, :].to_broadcast(bc), ALU.mult),
                     lambda: RED(f1[:, :, 0], a1[:, :, :], AX.X, ALU.max),
                     lambda: TT(oh1[:, :, :], a1[:, :, :], f1[:, :, :].to_broadcast(bc), ALU.is_equal)]
            if layer == 1:
                steps += [lambda: STT(flat(sh2[:, :, :]), flat(oh1[:, :, :]), BIG, flat(sh[:, :, :]), ALU.mult, ALU.add),
                          lambda: RED(r1[:, :, 0], sh2[:, :, :], AX.X, ALU.max),
                          lambda: TT(a2[:, :, :], sh2[:, :, :], r1[:, :, :].to_broadcast(bc), ALU.is_equal),
                          lambda: TT(a2[:, :, :], a2[:, :, :], p.first8[:, :, :].to_broadcast(bc), ALU.mult),
                          lambda: RED(r1[:, :, 0], a2[:, :, :], AX.X, ALU.max),
                          lambda: TT(oh2[:, :, :], a2[:, :, :], r1[:, :, :].to_broadcast(bc), ALU.is_equal),
                          lambda: TT(oh_b[:, :, :], oh1[:, :, :], oh2[:, :, :], ALU.add)]
            else:
                steps += [lambda: e.tensor_copy(oh_b[:, :, :], oh1[:, :, :])]
            assert len(steps) == RA
            steps += [(s_rexp, gg + 1),
                      lambda: RED(r1[:, :, 0], ex[:, :, :], AX.X, ALU.add)]
            if layer == 0:
                steps += [lambda: TS(r4[:, :, :], f1[:, :, :], -float(CAP), float((E + 1) * CAP), ALU.mult, ALU.add),
                          lambda: e.reciprocal(r2[:, :, :], r1[:, :, :]),
                          lambda: TS(r5[:, :, 0], tok, float(E * CAP), None, ALU.add)]
            else:
                steps += [lambda: e.reciprocal(r2[:, :, :], r1[:, :, :]),
                          lambda: TT(a2[:, :, :], ex[:, :, :], oh2[:, :, :], ALU.mult),
                          lambda: RED(r3[:, :, 0], a2[:, :, :], AX.X, ALU.add),
                          lambda: TT(r3[:, :, :], r3[:, :, :], r2[:, :, :], ALU.mult),
                          lambda: STT(r4[:, :, :], r2[:, :, :], 1e-8, r3[:, :, :], ALU.add, ALU.add),
                          lambda: e.reciprocal(r4[:, :, :], r4[:, :, :]),
                          lambda: TT(tails[:, slots, 0:1], r2[:, :, :], r4[:, :, :], ALU.mult),
                          lambda: TT(tails[:, slots, 1:2], r3[:, :, :], r4[:, :, :], ALU.mult),
                          lambda: TS(tails[:, slots, 2], tok, -float(TOK + T1), None, ALU.add),
                          lambda: e.tensor_copy(tails[:, slots, 3:4], f1[:, :, :])]
            steps += [(s_posr, gg + 1),
                      lambda: TT(pos[:, :, :], ranks[:, 0:G, :], p.next[:, :, :].to_broadcast(bc), ALU.add),
                      lambda: TT(p.next[:, :, :], p.next[:, :, :], ranks[:, G:G + 1, :], ALU.add),
                      lambda: TT(c1[:, :, :], pos[:, :, :], oh1[:, :, :], ALU.mult)]
            if layer == 0:
                steps += [lambda: RED(r3[:, :, 0], c1[:, :, :], AX.X, ALU.add),
                          lambda: TT(r4[:, :, :], r3[:, :, :], r4[:, :, :], ALU.is_lt),
                          lambda: TT(r3[:, :, :], r3[:, :, :], r5[:, :, :], ALU.subtract),
                          lambda: TT(r3[:, :, :], r3[:, :, :], r4[:, :, :], ALU.mult),
                          lambda: STT(r2[:, :, 0], r2[:, :, 0], -1.0, r4[:, :, 0], ALU.add, ALU.mult),
                          lambda: TS(p.factor0[:, gs], r2[:, :, 0], 1.0, None, ALU.add),
                          lambda: TT(p.row0[:, gs], r3[:, :, 0], r5[:, :, 0], ALU.add),
                          lambda: TT(rowf[:, slots, :], r3[:, :, :], r5[:, :, :], ALU.add)]
            else:
                steps += [lambda: TT(c2[:, :, :], pos[:, :, :], oh2[:, :, :], ALU.mult),
                          lambda: RED(rowf[:, slots, 0], c1[:, :, :], AX.X, ALU.add),
                          lambda: RED(rowf[:, slots, 1], c2[:, :, :], AX.X, ALU.add)]
            return Steps(e, s_route, gg, NR, steps)

        def maximum(e, k, t):
            wait(e, s_sim, t + 1)
            e.tensor_reduce(nmx[:, k % 2, :, 0], scores_ps(k).rearrange("p (h k) -> p h k", h=H), AX.X,
                            ALU.max, negate=True).then_inc(s_mx, 1)

        def dve_body(e, g):
            route = routing(e, g - 1, ((g - 1) % 2 if is_int(g) else (g + 1) % 2) * G) if okg(g - 1) else None
            for k in range(G):
                t = g * G + k
                hold = s_posr
                more = lambda: route.more(1, hold) if route and k >= 2 else None
                late = lambda: route.more(1, hold) if route and k >= 1 else None
                if ok(t + 2) and layer == 1:
                    maximum(e, k, t + 2)
                more()
                if ok(t):
                    wait(e, s_pThi, t + 1)
                    e.tensor_tensor(flat(pT_lo[:, :, :]), pT_ps(), flat(pT_hi[:, :, :]).bitcast(F32),
                                    ALU.subtract).then_inc(s_pTlo, 1)
                if ok(t + 2) and layer == 0:
                    maximum(e, k, t + 2)
                if k == 3 and route:
                    wait(e, s_pos, g)
                    e.tensor_copy(flat(ranks[:, :, :]), ps[:, O_BANK, RANKS]).then_inc(s_posr, 1)
                    hold = None
                more()
                if ok(t + 4):
                    wait(e, s_xThi, t + 5)
                    wait(e, s_xfTc, cap(t - 1))
                    e.tensor_tensor(flat(xT_lo[:, k % 2, :, :]), ps[:, X_BANK, 0:D],
                                    flat(xT_hi[:, k % 2, :, :]).bitcast(F32), ALU.subtract).then_inc(s_xTlo, 1)
                more()
                if ok(t + 1):
                    q = (k + 1) % 2
                    wait(e, s_exp, t + 2)
                    wait(e, s_p, t)
                    e.reciprocal(rc[:, q, :, :], sm[:, q, :, :]).then_inc(s_rcp, 1)
                more()
                if ok(t + 5):
                    q = (k + 1) % G
                    wait(e, s_rs1, t + 6)
                    wait(e, s_xT, t + 4)
                    e.tensor_scalar(xn[:, (k + 1) % 2, :], p.x[:, t + 5, :], mv1[:, q, 0:1], rs1[:, q:q + 1],
                                    ALU.subtract, ALU.mult).then_inc(s_xn, 1)
                more()
                if ok(t - 1):
                    wait(e, s_rs2, t)
                    wait(e, s_xfT, t - 2)
                    e.tensor_scalar(xf[:, (k + 1) % 2, :], p.x[:, t - 1, :], mv[:, t - 1, 0:1], col(rs2, t - 1),
                                    ALU.subtract, ALU.mult).then_inc(s_xf, 1)
                    e.scalar_tensor_tensor(col(nb2, t - 1), mv[:, t - 1, 0:1], -1.0, col(rs2, t - 1),
                                           ALU.mult, ALU.mult).then_inc(s_nb2, 1)
                more()
                q = (k + 2) % G
                x6 = p.x[:, t + 6, :] if ok(t + 6) else None
                if ok(t + 6) and layer == 1:
                    wait(e, s_got[q], 16 * (g + (2 if k < 2 else 3)))
                    e.scalar_tensor_tensor(x6, got[:, q, :], col(p.factor0, t + 6), x6, ALU.mult, ALU.add).then_inc(s_cmb, 1)
                more()
                if ok(t):
                    wait(e, s_out, t + 1)
                    e.tensor_tensor(p.x[:, t, :], ps[:, O_BANK, 0:D], p.x[:, t, :], ALU.add).then_inc(s_res, 1)
                if ok(t - 2):
                    wait(e, s_lgp, t - 1)
                    e.tensor_copy(lg[:, (k - 2) % G, :], ps[:, X_BANK, LOGITS]).then_inc(s_lg, 1)
                if k == 1 and route:
                    route.add_wait(s_lg, t - 1)
                late()
                if ok(t + 6):
                    if layer == 1:
                        wait(e, s_cmb, t + 7)
                        land(e, t)
                    e.bn_stats(stats[:, 0, :], x6).then_inc(s_ch1, 1)
                late()
                if ok(t):
                    wait(e, s_res, t + 1)
                    land(e, t)
                    e.bn_stats(stats[:, 1, :], p.x[:, t, :]).then_inc(s_ch2, 1)
                late()
                if ok(t + 6):
                    wait(e, s_ch1, t + 7)
                    land(e, t)
                    e.bn_aggr(mv1[:, q, :], stats[:, 0, :]).then_inc(s_st1, 1)
                late()
                if ok(t):
                    wait(e, s_ch2, t + 1)
                    land(e, t)
                    e.bn_aggr(mv2[:, k, :], stats[:, 1, :]).then_inc(s_st2, 1)
                if k == 3 and route:
                    route.more(NR)
                    assert route.j == NR, route.j

        def plan(q):
            q.tensor_copy(tail_i[:, :], p.next[:, 0, :]).then_inc(s_tab, 1)
            c = Chain(q, s_tb, 0, 28)
            c(q.scalar_tensor_tensor(tiles_a[:, 0, :], p.expert8[:, 0, :], -float(ROOM), p.next[:, 0, :],
                                     ALU.mult, ALU.add))
            c(q.tensor_scalar(tiles_a[:, 0, :], tiles_a[:, 0, :], float(T1 - 1), None, ALU.add))
            c(q.tensor_copy(tiles_i[:, 0, :], tiles_a[:, 0, :]))
            c(q.tensor_scalar(tiles_i[:, 0, :], tiles_i[:, 0, :], 8, None, ALU.arith_shift_right))
            c(q.tensor_copy(base[:, 0, :], tiles_i[:, 0, :]))
            c(q.tensor_copy(tiles[:, 0, 0:1], base[:, 0, 0:1]))
            for e in range(1, E):
                c(q.tensor_tensor(tiles[:, 0, e:e + 1], tiles[:, 0, e - 1:e], base[:, 0, e:e + 1], ALU.add))
            c(q.tensor_tensor(base[:, 0, :], tiles[:, 0, :], base[:, 0, :], ALU.subtract))
            c(q.tensor_scalar(base[:, 0, :], base[:, 0, :], -float(T1), None, ALU.mult))
            c(q.scalar_tensor_tensor(base[:, 0, :], p.expert8[:, 0, :], float(ROOM), base[:, 0, :], ALU.mult, ALU.add))
            q.wait_ge(s_num, 1)
            c(q.tensor_copy(num[:, :, 0], num_i[:, :]))
            c(q.tensor_tensor(cmp[:, :, :], num[:, :, :].to_broadcast([P, NT1, E]),
                              tiles[:, :, :].to_broadcast([P, NT1, E]), ALU.is_ge))
            c(q.tensor_reduce(p.own[:, :, 0], cmp[:, :, :], AX.X, ALU.add))
            c(q.tensor_tensor(cmp[:, :, :], p.own[:, :, :].to_broadcast([P, NT1, E]),
                              p.expert8[:, :, :].to_broadcast([P, NT1, E]), ALU.is_equal))
            c(q.tensor_tensor(cmp[:, :, :], cmp[:, :, :], base[:, :, :].to_broadcast([P, NT1, E]), ALU.mult))
            c(q.tensor_reduce(first[:, :, 0], cmp[:, :, :], AX.X, ALU.add))
            c(q.scalar_tensor_tensor(first[:, :, 0], num[:, :, 0], float(T1), first[:, :, 0], ALU.mult, ALU.add))
            c(q.tensor_scalar(ra[:, :, :], p.own[:, :, :], float(E), None, ALU.is_equal))
            c(q.tensor_scalar(rb[:, :, :], first[:, :, :], -1.0, float(IDLE_ROW), ALU.mult, ALU.add))
            c(q.tensor_tensor(rb[:, :, :], rb[:, :, :], ra[:, :, :], ALU.mult))
            q.tensor_tensor(p.tab[:, 0, :], first[:, :, 0], rb[:, :, 0], ALU.add)
            q.tensor_scalar(p.tab[:, 1, :], p.own[:, :, 0], float(E - 1), None, ALU.min).then_inc(s_tab, 1)
            c(q.tensor_scalar(p.own[:, :, 0], p.own[:, :, 0], -1.0, float(E), ALU.mult, ALU.add))
            for r in range(TC):
                q.tensor_scalar(p.spare[:, r, :], p.token[:, r:r + 1], float(TOK), None, ALU.add)
                last = q.tensor_scalar(p.shift[:, r, :], p.token[:, r:r + 1], -1.0, float(T1), ALU.mult, ALU.add)
            c(last)
            c.end()

        @block.vector
        def _(e):
            if layer == 0:
                e.wait_ge(p.s_x, 16 * 4)
            else:
                e.memset(zero[:, :], 0.0).then_inc(s_zero, 1)
            run(e, lambda g: dve_body(e, g))
            if layer == 1:
                plan(e)


def experts_capacity(p, ins):
    nc, ps = p.nc, p.psum
    FC, TC = F0 // P, CAP // P
    HALVES = ((0, 3), (3, 2))
    n = "E0_"
    with ExitStack() as st:
        w1, w2 = p.w1, p.w2
        w1_hi, w1_lo = (p.sb(st, n + x, [P, 2, KC, F0], F32R) for x in ("w1_hi", "w1_lo"))
        w2_hi, w2_lo = (p.sb(st, n + x, [P, 2, FC, D], F32R) for x in ("w2_hi", "w2_lo"))
        xin = p.sb(st, n + "xin", [P, TC, D])
        xT_hi, xT_lo = (p.sb(st, n + x, [P, KC, CAP], F32R) for x in ("xT_hi", "xT_lo"))
        h_hi, h_lo = (p.sb(st, n + x, [P, 2, FC, 3 * P], F32R) for x in ("h_hi", "h_lo"))
        y = p.sb(st, n + "y", [P, 2, 3, D])
        S = lambda name: p.sem(n + name)
        s_w1, s_w2, s_x = S("w1_loaded"), S("w2_loaded"), S("x_loaded")
        s_w1hi, s_w1lo, s_w2hi, s_w2lo, s_used = S("w1_hi"), S("w1_lo"), S("w2_hi"), S("w2_lo"), S("weights_used")
        s_xT, s_xThi, s_xTlo, s_up = S("xT"), S("xT_hi"), S("xT_lo"), S("up")
        s_hhi, s_hlo, s_dn, s_y, s_st = S("h_hi"), S("h_lo"), S("down"), S("y_copied"), [S("y_stored0"), S("y_stored1")]
        w1_d = ins["w1"].rearrange("e (c p) f -> p e c f", p=P)
        w2_d = ins["w2"].rearrange("e (m p) d -> p e m d", p=P)
        rows = p.d0[0:E * CAP, :].rearrange("(e c p) d -> p e c d", p=P, c=TC)
        UP_BANK, Y_BANK = 0, 6
        X_BANK = 0

        def pairs(eng, body):
            body(0, 0)
            body(1, 1)
            with eng.Fori(1, E // 2 - 1) as j:
                body(2 * j, 0)
                body(2 * j + 1, 1)
            body(E - 2, 0)
            body(E - 1, 1)

        def load(q, e):
            if not is_int(e) or e > 0:
                wait(q, s_w1lo, e)
                q.dma_start(w1[:, :, :], w1_d[:, e, :, :]).then_inc(s_w1, 16)
                wait(q, s_w2lo, e)
                q.dma_start(w2[:, :, :], w2_d[:, e, :, :]).then_inc(s_w2, 16)
            wait(q, s_xT, TC * e)
            q.dma_start(xin[:, :, :], rows[:, e, :, :]).then_inc(s_x, 16)

        with nc.Block() as block:
            @block.sync
            def _(q):
                load(q, 0)
                def body(e, par, last=False):
                    if not last:
                        load(q, e + 1)
                    for h, (c0, cn) in enumerate(HALVES):
                        q.wait_ge(s_y, TC * e + c0 + cn)
                        q.dma_start(rows[:, e, c0:c0 + cn, :], y[:, h, 0:cn, :]).then_inc(s_st[h], 16)
                body(0, 0)
                with q.Fori(1, E - 1) as e:
                    body(e, 0)
                body(E - 1, 0, True)
                for h in range(2):
                    q.wait_ge(s_st[h], 16 * E)

            def transposes(q, e):
                q.wait_ge(s_x, 16 * (e + 1))
                wait(q, s_hlo, 2 * FC * e)
                for c in range(TC):
                    for kc in range(KC):
                        mm = q.transpose(ps[:, X_BANK + c, kc * P:(kc + 1) * P],
                                         xin[:, c, kc * P:(kc + 1) * P], p.ident[:, :])
                    mm.then_inc(s_xT, 1)

            @block.tensor
            def _(q):
                transposes(q, 0)

                def up(e, par, h):
                    c0, cn = HALVES[h]
                    q.wait_ge(s_xTlo, TC * e + TC)
                    if h == 0:
                        q.wait_ge(s_w1lo, e + 1)
                    for m in range(FC):
                        i = (2 * e + h) * FC + m
                        wait(q, s_hlo, i - 3)
                        bank = ps[:, UP_BANK + m % 4, 0:cn * P]
                        k = 0
                        for c in range(KC):
                            for a, x in ((w1_hi, xT_hi), (w1_hi, xT_lo), (w1_lo, xT_hi)):
                                mm = q.matmul(bank, a[:, par, c, m * P:(m + 1) * P], x[:, c, c0 * P:(c0 + cn) * P],
                                              start=(k == 0), stop=(k == 3 * KC - 1))
                                k += 1
                        mm.then_inc(s_up, 1)

                def down(e, par, h):
                    c0, cn = HALVES[h]
                    if h == 0:
                        q.wait_ge(s_w2lo, e + 1)
                    q.wait_ge(s_hlo, (2 * e + h + 1) * FC)
                    for c in range(cn):
                        i = TC * e + c0 + c
                        wait(q, s_y, i - 1)
                        bank = ps[:, Y_BANK + (c0 + c + par) % 2, 0:D]
                        k = 0
                        for m in range(FC):
                            for a, w in ((h_hi, w2_hi), (h_lo, w2_hi), (h_hi, w2_lo)):
                                mm = q.matmul(bank, a[:, h, m, c * P:(c + 1) * P], w[:, par, m, :],
                                              start=(k == 0), stop=(k == 3 * FC - 1))
                                k += 1
                        mm.then_inc(s_dn, 1)

                def body(e, par, last=False):
                    up(e, par, 0)
                    up(e, par, 1)
                    down(e, par, 0)
                    if not last:
                        transposes(q, e + 1)
                    down(e, par, 1)
                pairs(q, lambda e, par: body(e, par, is_int(e) and e == E - 1))

            @block.scalar
            def _(q):
                def split_w1(e, par):
                    wait(q, s_w1, 16 * e)
                    wait(q, s_dn, TC * (e - 1))
                    q.activation(w1_hi[:, par, :, :], w1[:, :, :], ACT.Copy).then_inc(s_w1hi, 1)

                def split_w2(e, par):
                    wait(q, s_w2, 16 * e)
                    q.activation(w2_hi[:, par, :, :], w2[:, :, :], ACT.Copy).then_inc(s_w2hi, 1)

                def split_x(e):
                    for c in range(TC):
                        q.wait_ge(s_xT, TC * e + c + 1)
                        if c == 0:
                            wait(q, s_up, 2 * FC * e)
                        q.activation(xT_hi[:, :, c * P:(c + 1) * P],
                                     ps[:, X_BANK + c, 0:D].rearrange("p (k t) -> p k t", k=KC),
                                     ACT.Copy).then_inc(s_xThi, 1)

                def hidden(e, h):
                    cn = HALVES[h][1]
                    for m in range(FC):
                        q.wait_ge(s_up, (2 * e + h) * FC + m + 1)
                        if m == 0:
                            wait(q, s_dn, TC * (e - 1) + sum(HALVES[h]))
                        q.activation(h_hi[:, h, m, 0:cn * P], ps[:, UP_BANK + m % 4, 0:cn * P], ACT.Relu).then_inc(s_hhi, 1)

                split_w1(0, 0)
                split_x(0)
                split_w2(0, 0)

                def body(e, par, last=False):
                    hidden(e, 0)
                    hidden(e, 1)
                    if not last:
                        split_w1(e + 1, 1 - par)
                        split_w2(e + 1, 1 - par)
                        split_x(e + 1)
                pairs(q, lambda e, par: body(e, par, is_int(e) and e == E - 1))

            @block.vector
            def _(q):
                def split_w(e, par):
                    q.wait_ge(s_w1hi, e + 1)
                    q.tensor_tensor(w1_lo[:, par, :, :], w1[:, :, :], w1_hi[:, par, :, :].bitcast(F32),
                                    ALU.subtract).then_inc(s_w1lo, 1)

                def split_x(e):
                    for c in range(TC):
                        q.wait_ge(s_xThi, TC * e + c + 1)
                        q.tensor_tensor(xT_lo[:, :, c * P:(c + 1) * P],
                                        ps[:, X_BANK + c, 0:D].rearrange("p (k t) -> p k t", k=KC),
                                        xT_hi[:, :, c * P:(c + 1) * P].bitcast(F32), ALU.subtract).then_inc(s_xTlo, 1)

                def hidden(e, h):
                    cn = HALVES[h][1]
                    for m in range(FC):
                        q.wait_ge(s_hhi, (2 * e + h) * FC + m + 1)
                        q.scalar_tensor_tensor(h_lo[:, h, m, 0:cn * P], ps[:, UP_BANK + m % 4, 0:cn * P], 0.0,
                                               h_hi[:, h, m, 0:cn * P].bitcast(F32), ALU.max,
                                               ALU.subtract).then_inc(s_hlo, 1)

                def outputs(e, par, h):
                    c0, cn = HALVES[h]
                    wait(q, s_st[h], 16 * e)
                    for c in range(cn):
                        q.wait_ge(s_dn, TC * e + c0 + c + 1)
                        if not is_int(e):
                            q.sem_inc(p.s_land, 1)
                        q.tensor_copy(y[:, h, c, :], ps[:, Y_BANK + (c0 + c + par) % 2, 0:D]).then_inc(s_y, 1)

                split_w(0, 0)
                split_x(0)

                def body(e, par, last=False):
                    hidden(e, 0)
                    hidden(e, 1)
                    if not last:
                        split_w(e + 1, 1 - par)
                    outputs(e, par, 0)
                    if not last:
                        split_x(e + 1)
                    outputs(e, par, 1)
                pairs(q, lambda e, par: body(e, par, is_int(e) and e == E - 1))

            @block.gpsimd
            def _(q):
                def split_w(e, par):
                    q.wait_ge(s_w2hi, e + 1)
                    q.tensor_tensor(w2_lo[:, par, :, :], w2[:, :, :], w2_hi[:, par, :, :].bitcast(F32),
                                    ALU.subtract).then_inc(s_w2lo, 1)
                pairs(q, split_w)


def experts_top2(p, ins):
    nc, ps = p.nc, p.psum
    FC, TC = F1 // P, T1 // P
    NM = 6
    n = "E1_"
    with ExitStack() as st:
        wg, wv = (p.sb(st, n + x, [P, 2, KC, F1]) for x in ("wg", "wv"))
        w2 = p.sb(st, n + "w2", [P, 2, FC, D])
        wg_hi, wg_lo, wv_hi, wv_lo = (p.sb(st, n + x, [P, 2, KC, F1], F32R) for x in ("wg_hi", "wg_lo", "wv_hi", "wv_lo"))
        w2_hi, w2_lo = (p.sb(st, n + x, [P, 2, FC, D], F32R) for x in ("w2_hi", "w2_lo"))
        xin = p.sb(st, n + "xin", [P, 2, TC, DW])
        xT_hi, xT_lo = (p.sb(st, n + x, [P, KC, T1], F32R) for x in ("xT_hi", "xT_lo"))
        sg = p.sb(st, n + "sg", [P, FC, T1])
        hf = p.sb(st, n + "hf", [P, FC, T1])
        h_hi, h_lo = (p.sb(st, n + x, [P, 2, FC, T1], F32R) for x in ("h_hi", "h_lo"))
        y = p.sb(st, n + "y", [P, 2, TC, D])
        wt, dest = p.sb(st, n + "wt", [P, 2, TC, 1]), p.sb(st, n + "dest", [P, 2, TC, 1], I32)
        ma, mb = (p.sb(st, n + x, [P, TC, 1]) for x in ("ma", "mb"))
        S = lambda name: p.sem(n + name)
        s_w, s_w2, s_x = ([S(f"{x}_loaded{j}") for j in range(2)] for x in ("w1", "w2", "x"))
        s_w2hi, s_w2lo = S("w2_hi"), S("w2_lo")
        s_whi, s_wlo, s_xT, s_xThi, s_xTlo = S("w_hi"), S("w_lo"), S("xT"), S("xT_hi"), S("xT_lo")
        s_up, s_sg, s_hf, s_hhi, s_hlo, s_dn, s_y = (S(x) for x in ("up", "silu", "h", "h_hi", "h_lo", "down", "y_scaled"))
        s_mt, s_add = S("meta_steps"), S("rows_added")
        UP_BANK, X_BANK, Y_BANK = 0, 4, 6
        d1 = p.d1
        wd = [ins[x].rearrange("e (c p) f -> p e c f", p=P) for x in ("w11", "w12")]
        w2_d = ins["w22"].rearrange("e (m p) d -> p e m d", p=P)

        def nth(i):
            return (i + 2) // 2 if is_int(i) else (i + 2) >> 1

        def tiles_loop(eng, body):
            body(0, 0, False)
            body(1, 1, False)
            with eng.Fori(1, NT1 // 2) as j:
                body(2 * j, 0, False)
                body(2 * j + 1, 1, False)
            body(NT1 - 1, 0, True)
        assert NT1 % 2 == 1

        def land(eng, i):
            if not is_int(i):
                eng.sem_inc(p.s_land, 1)

        with nc.Block() as block:
            @block.sync
            def _(q):
                def expert(i):
                    return q.value_load(p.tab[0:1, 1, i:i + 1] if is_int(i) else p.tab[0:1, 1, bass.ds(i, 1)], min_val=0, max_val=E - 1)

                def load_w(i, par):
                    e = expert(i)
                    wait(q, s_wlo, 2 * (i - 1))
                    land(q, i)
                    q.dma_start(wg[:, par, :, :], wd[0][:, e, :, :]).then_inc(s_w[par], 16)
                    q.dma_start(wv[:, par, :, :], wd[1][:, e, :, :]).then_inc(s_w[par], 16)

                def load_w2(i, par):
                    e = expert(i)
                    wait(q, s_w2lo, i - 1)
                    land(q, i)
                    q.dma_start(w2[:, par, :, :], w2_d[:, e, :, :]).then_inc(s_w2[par], 16)

                def load_x(i, par):
                    r = q.value_load(p.tab[0:1, 0, i:i + 1] if is_int(i) else p.tab[0:1, 0, bass.ds(i, 1)], min_val=0, max_val=IDLE_ROW)
                    wait(q, s_mt, NM * (i - 1))
                    wait(q, s_xT, i - 1)
                    land(q, i)
                    q.dma_start(xin[:, par, :, :],
                                d1[bass.ds(r, T1), :].rearrange("(c p) d -> p c d", p=P)).then_inc(s_x[par], 16)
                load_w(0, 0)
                load_x(0, 0)
                load_w2(0, 0)

                def body(i, par, last):
                    if not last:
                        load_w(i + 1, 1 - par)
                        load_x(i + 1, 1 - par)
                        load_w2(i + 1, 1 - par)
                tiles_loop(q, body)

            @block.tensor
            def _(q):
                def transposes(i, par):
                    q.wait_ge(s_x[par], 16 * nth(i))
                    wait(q, s_xTlo, i)
                    for c in range(TC):
                        for kc in range(KC):
                            mm = q.transpose(ps[:, X_BANK + kc, c * P:(c + 1) * P],
                                             xin[:, par, c, kc * P:(kc + 1) * P], p.ident[:, :])
                    mm.then_inc(s_xT, 1)

                def down(i, par):
                    wait(q, s_w2lo, i + 1)
                    wait(q, s_hlo, (i + 1) * FC)
                    for c in range(TC):
                        wait(q, s_y, TC * i + c - 1)
                        k = 0
                        for m in range(FC):
                            for a, w in ((h_hi, w2_hi), (h_lo, w2_hi), (h_hi, w2_lo)):
                                mm = q.matmul(ps[:, Y_BANK + c, 0:D], a[:, par, m, c * P:(c + 1) * P], w[:, par, m, :],
                                              start=(k == 0), stop=(k == 3 * FC - 1))
                                k += 1
                        mm.then_inc(s_dn, 1)

                def body(i, par, last):
                    q.wait_ge(s_xTlo, i + 1)
                    q.wait_ge(s_wlo, 2 * i + 2)
                    for m in range(FC):
                        wait(q, s_hf, i * FC + m - 3)
                        for half, (hi, lo) in enumerate(((wg_hi, wg_lo), (wv_hi, wv_lo))):
                            bank = ps[:, UP_BANK + m, half * T1:(half + 1) * T1]
                            k = 0
                            for c in range(KC):
                                for a, x in ((hi, xT_hi), (hi, xT_lo), (lo, xT_hi)):
                                    mm = q.matmul(bank, a[:, par, c, m * P:(m + 1) * P], x[:, c, :],
                                                  start=(k == 0), stop=(k == 3 * KC - 1))
                                    k += 1
                        mm.then_inc(s_up, 1)
                    if not last:
                        transposes(i + 1, 1 - par)
                    if not is_int(i) or i > 0:
                        down(i - 1, 1 - par)
                    if last:
                        down(i, par)
                transposes(0, 0)
                tiles_loop(q, body)

            @block.scalar
            def _(q):
                def split_w(i, par, j):
                    if j == 0:
                        q.wait_ge(s_w[par], 32 * nth(i))
                        wait(q, s_up, FC * (i - 1))
                    hi, w = ((wg_hi, wg), (wv_hi, wv))[j]
                    q.activation(hi[:, par, :, :], w[:, par, :, :], ACT.Copy).then_inc(s_whi, 1)

                def split_w2(i, par):
                    q.wait_ge(s_w2[par], 16 * nth(i))
                    wait(q, s_dn, TC * (i - 1))
                    q.activation(w2_hi[:, par, :, :], w2[:, par, :, :], ACT.Copy).then_inc(s_w2hi, 1)

                def split_x(i, par):
                    q.wait_ge(s_xT, i + 1)
                    q.activation(xT_hi[:, :, :], ps[:, X_BANK:X_BANK + KC, 0:T1], ACT.Copy).then_inc(s_xThi, 1)

                def hidden_hi(i, par, m):
                    q.wait_ge(s_hf, i * FC + m + 1)
                    if m == 0:
                        wait(q, s_dn, TC * (i - 1))
                    q.activation(h_hi[:, par, m, :], hf[:, m, :], ACT.Copy).then_inc(s_hhi, 1)

                def body(i, par, last):
                    for m in range(FC):
                        q.wait_ge(s_up, i * FC + m + 1)
                        wait(q, s_hf, (i - 1) * FC + m + 1)
                        q.activation(sg[:, m, :], ps[:, UP_BANK + m, 0:T1], ACT.Silu).then_inc(s_sg, 1)
                        if m < 2 and not last:
                            split_w(i + 1, 1 - par, m)
                        if m == 2:
                            split_w2(i, par)
                        if 0 < m < 3:
                            hidden_hi(i, par, m - 1)
                    if not last:
                        split_x(i + 1, 1 - par)
                    for m in (2, 3):
                        hidden_hi(i, par, m)
                for j in range(2):
                    split_w(0, 0, j)
                split_x(0, 0)
                tiles_loop(q, body)

            @block.vector
            def _(q):
                def split_w(i, par, j):
                    hi, lo, w = ((wg_hi, wg_lo, wg), (wv_hi, wv_lo, wv))[j]
                    q.wait_ge(s_whi, 2 * i + j + 1)
                    q.tensor_tensor(lo[:, par, :, :], w[:, par, :, :], hi[:, par, :, :].bitcast(F32),
                                    ALU.subtract).then_inc(s_wlo, 1)

                def split_w2(i, par):
                    q.wait_ge(s_w2hi, i + 1)
                    q.tensor_tensor(w2_lo[:, par, :, :], w2[:, par, :, :], w2_hi[:, par, :, :].bitcast(F32),
                                    ALU.subtract).then_inc(s_w2lo, 1)

                def split_x(i, par):
                    q.wait_ge(s_xThi, i + 1)
                    q.tensor_tensor(xT_lo[:, :, :], ps[:, X_BANK:X_BANK + KC, 0:T1], xT_hi[:, :, :].bitcast(F32),
                                    ALU.subtract).then_inc(s_xTlo, 1)

                def meta(i, par):
                    m = lambda j: xin[:, par, :, D + j:D + j + 1]
                    own_i = p.own[:, i:i + 1, 0] if is_int(i) else p.own[:, bass.ds(i, 1), 0]
                    TT, STT = q.tensor_tensor, q.scalar_tensor_tensor
                    return Steps(q, s_mt, i, NM, [
                        (s_x[par], 16 * nth(i)),
                        lambda: TT(ma[:, :, :], m(0), m(1), ALU.subtract),
                        lambda: STT(ma[:, :, 0], xin[:, par, :, D + 3], own_i, ma[:, :, 0], ALU.is_equal, ALU.mult),
                        lambda: TT(wt[:, par, :, :], ma[:, :, :], m(1), ALU.add),
                        lambda: STT(mb[:, :, 0], xin[:, par, :, D + 2], 0.0, p.shift[:, :, 0], ALU.is_lt, ALU.mult),
                        lambda: TT(mb[:, :, :], mb[:, :, :], p.spare[:, :, :], ALU.add),
                        lambda: TT(mb[:, :, :], mb[:, :, :], m(2), ALU.add)])

                def outputs(i, par):
                    for c in range(TC):
                        wait(q, s_dn, TC * i + c + 1)
                        wait(q, s_mt, NM * (i + 1))
                        q.tensor_scalar(y[:, par, c, :], ps[:, Y_BANK + c, 0:D], wt[:, par, c, :], None,
                                        ALU.mult).then_inc(s_y, 1)

                def body(i, par, last):
                    small = meta(i, par)
                    for m in range(FC):
                        q.wait_ge(s_sg, i * FC + m + 1)
                        wait(q, s_hlo, (i - 1) * FC + m + 1)
                        q.tensor_tensor(hf[:, m, :], ps[:, UP_BANK + m, T1:2 * T1], sg[:, m, :],
                                        ALU.mult).then_inc(s_hf, 1)
                        small.more(1)
                        if m < 2 and not last:
                            split_w(i + 1, 1 - par, m)
                        if m == 2:
                            split_w2(i, par)
                        small.more(1)
                    if not last:
                        split_x(i + 1, 1 - par)
                    if not is_int(i) or i > 0:
                        outputs(i - 1, 1 - par)
                    wait(q, s_mt, NM * (i + 1))
                    wait(q, s_add, 16 * TC * (i - 1))
                    q.tensor_copy(dest[:, par, :, :], mb[:, :, :])
                    if last:
                        outputs(i, par)
                for j in range(2):
                    split_w(0, 0, j)
                split_x(0, 0)
                tiles_loop(q, body)

            @block.gpsimd
            def _(q):

                def add(i, par):
                    for c in range(TC):
                        wait(q, s_y, TC * i + c + 1)
                        wait(q, s_add, 16 * (TC * i + c))
                        land(q, i)
                        q.indirect_dma_start(p.out[:, :], bass.IndirectOffsetOnAxis(ap=dest[:, par, c, :], axis=0),
                                             y[:, par, c, :], None, compute_op=ALU.add).then_inc(s_add, 16)

                def body(i, par, last):
                    for m in range(FC):
                        q.wait_ge(s_hhi, i * FC + m + 1)
                        q.tensor_tensor(h_lo[:, par, m, :], hf[:, m, :], h_hi[:, par, m, :].bitcast(F32),
                                        ALU.subtract).then_inc(s_hlo, 1)
                    if not is_int(i) or i > 0:
                        add(i - 1, 1 - par)
                    if last:
                        add(i, par)
                tiles_loop(q, body)
                q.wait_ge(s_add, 16 * TC * NT1)


def build(nc, ins, out):
    p = Program(nc)
    p.out = out
    p.d0 = nc.dram_tensor("rows0", [D0_ROWS, D], F32, kind="Internal").ap()
    p.d1 = nc.dram_tensor("rows1", [D1_ROWS, DW], F32, kind="Internal").ap()
    p.s_land = p.sem("landing")
    first = ExitStack()
    constants(p, first)
    for layer in range(2):
        with ExitStack() as st:
            mats = attention_setup(p, layer, ins, st)
            attention(p, layer, ins, mats, st)
        if layer == 0:
            p.phase()
            experts_capacity(p, ins)
            first.close()
            p.phase()
        else:
            p.phase()
            experts_top2(p, ins)
    p.keep.close()


def kernel(x, ctx_768, mask_BxS2_bk0, L0_xattn_W_q, L0_xattn_W_k, L0_xattn_W_v, L0_xattn_W_o, L0_xattn_b_o,
           L0_ffn_Wr, L0_ffn_W1, L0_ffn_W2, L1_xattn_w_q, L1_xattn_w_k, L1_xattn_w_v, L1_xattn_w_o,
           L1_xattn_b_o, L1_ffn_Wg, L1_ffn_W11, L1_ffn_W12, L1_ffn_W2):
    import concourse.bacc as bacc
    from concourse.bass_utils import run_bass_kernel_spmd as run

    a = lambda v: np.ascontiguousarray(np.asarray(v))
    arrays = {
        "x": a(x).reshape(TOK, D),
        "ctxT": a(a(ctx_768).reshape(B * KEYS, CTX).T),
        "mask": a(mask_BxS2_bk0).reshape(1, B * KEYS),
        "wqT0": a(a(L0_xattn_W_q).T), "wk0": a(L0_xattn_W_k), "wv0": a(L0_xattn_W_v), "wo0": a(L0_xattn_W_o),
        "bo0": a(L0_xattn_b_o).reshape(1, D),
        "wr0": a(L0_ffn_Wr), "w1": a(L0_ffn_W1), "w2": a(L0_ffn_W2),
        "wqT1": a(a(L1_xattn_w_q).T), "wk1": a(L1_xattn_w_k), "wv1": a(L1_xattn_w_v), "wo1": a(L1_xattn_w_o),
        "bo1": a(L1_xattn_b_o).reshape(1, D),
        "wr1": a(L1_ffn_Wg), "w11": a(L1_ffn_W11), "w12": a(L1_ffn_W12), "w22": a(L1_ffn_W2),
    }
    nc = bacc.Bacc("TRN2", target_bir_lowering=False, num_devices=1)
    ins = {name: nc.dram_tensor("in_" + name, v.shape, mybir.dt.from_np(v.dtype), kind="ExternalInput").ap()
           for name, v in arrays.items()}
    out = nc.dram_tensor("out", (TOK + T1, D), F32, kind="ExternalOutput").ap()
    build(nc, ins, out)
    r = run(nc, [{"in_" + name: v for name, v in arrays.items()}], core_ids=[0])
    return r.results[0]["out"][0:TOK].reshape(B, SEQ, D)
```
